# Optimizing a Trainium2 kernel written in Bass

```python
import numpy as np
import jax
import jax.numpy as jnp

def _softmax(x, axis=-1):
    return jax.nn.softmax(x, axis=axis)

def _gelu(x):
    return jax.nn.gelu(x, approximate=True)

def _silu(x):
    return jax.nn.silu(x)

def _sigmoid(x):
    return jax.nn.sigmoid(x)

def _layernorm(x, axis=-1, eps=1e-05):
    m = jnp.mean(x, axis=axis, keepdims=True)
    v = jnp.var(x, axis=axis, keepdims=True)
    return (x - m) / jnp.sqrt(v + eps)

def _scatter_add(tgt, idx, src, axis=0):
    return tgt.at[idx].add(src)

def _segment_sum(src, seg, n):
    return jax.ops.segment_sum(src, seg, n)
kernel_name = 'mk_seq_postln_d2_jaxref_r4_35d30b'

def setup_inputs(seed: int=0):
    np.random.seed(seed)
    _w = jnp.asarray

    def _L0_attn_setup():
        import jax, jax.numpy as jnp
        import numpy as np
        D_MODEL = 512
        D_STATE = 16
        D_CONV = 4
        EXPAND = 2
        D_INNER = EXPAND * D_MODEL
        HEAD_DIM = 64
        N_HEADS = D_INNER // HEAD_DIM
        N_GROUPS = 1
        CONV_DIM = D_INNER + 2 * N_GROUPS * D_STATE
        IN_DIM = D_INNER + CONV_DIM + N_HEADS
        BATCH, SEQ = (2, 1024)
        EPS = 1e-05
        key = jax.random.key(seed)
        ks = jax.random.split(key, 8)
        s = 0.02
        return {'hidden_states': jax.random.normal(ks[0], (BATCH, SEQ, D_MODEL), jnp.float32), 'W_in': jax.random.normal(ks[1], (D_MODEL, IN_DIM), jnp.float32) * s, 'conv_w': jax.random.normal(ks[2], (CONV_DIM, D_CONV), jnp.float32) * s, 'conv_b': jnp.zeros((CONV_DIM,), jnp.float32), 'A_log': jnp.log(jax.random.uniform(ks[3], (N_HEADS,), jnp.float32, 1.0, 16.0)), 'D_skip': jnp.ones((N_HEADS,), jnp.float32), 'dt_bias': jnp.ones((N_HEADS,), jnp.float32), 'norm_w': jnp.ones((D_INNER,), jnp.float32), 'W_out': jax.random.normal(ks[4], (D_INNER, D_MODEL), jnp.float32) * s}
    _L0_attn_in = _L0_attn_setup()

    def _L0_ffn_setup():
        import jax, jax.numpy as jnp
        import numpy as np
        EPS = 1e-07
        CURVATURE = 1.0
        MAX_NORM_RATIO = 0.99
        B, L, N, K = (4, 512, 512, 512)

        def _ternary_init(key, n, k):
            rand = jax.random.normal(key, (n, k), dtype=jnp.float32)
            threshold = 0.5 * jnp.mean(jnp.abs(rand))
            return jnp.where(rand > threshold, 1.0, jnp.where(rand < -threshold, -1.0, 0.0)).astype(jnp.float32)
        key = jax.random.key(seed)
        kx, kw = jax.random.split(key)
        x = jax.random.normal(kx, (B, L, N), dtype=jnp.float32)
        weight = _ternary_init(kw, N, K)
        scale = jnp.full((K,), 1.0 / np.sqrt(N), dtype=jnp.float32)
        return {'x': x, 'weight': weight, 'scale': scale}
    _L0_ffn_in = _L0_ffn_setup()

    def _L1_attn_setup():
        import jax, jax.numpy as jnp
        import numpy as np
        B, T, D, L, K = (4, 512, 512, 512, 4)

        def _reference_tuple_inner(x, w_y, b_y, w_x, b_x, conv_w, conv_b, a_param, w_ig, b_ig, w_ag, b_ag, w_out, b_out):
            Tn = x.shape[1]
            y = jax.nn.gelu(jnp.einsum('btd,dl->btl', x, w_y) + b_y, approximate=False)
            xb = jnp.einsum('btd,dl->btl', x, w_x) + b_x
            xp = jnp.pad(xb, ((0, 0), (K - 1, 0), (0, 0)))
            conv = conv_b
            for k in range(K):
                conv = conv + conv_w[k] * xp[:, k:k + Tn]
            gate_x = jax.nn.sigmoid(jnp.einsum('btl,lm->btm', conv, w_ig) + b_ig)
            gate_a = jax.nn.sigmoid(jnp.einsum('btl,lm->btm', conv, w_ag) + b_ag)
            log_a = -8.0 * gate_a * jax.nn.softplus(a_param)
            a = jnp.exp(log_a)
            mult = jnp.sqrt(1.0 - jnp.exp(2.0 * log_a))
            reset = (jnp.arange(Tn) == 0)[None, :, None]
            a = jnp.where(reset, 0.0, a)
            mult = jnp.where(reset, 1.0, mult)
            nx = gate_x * conv * mult

            def step(h, inp):
                a_t, x_t = inp
                h = a_t * h + x_t
                return (h, h)
            h0 = jnp.zeros((x.shape[0], a.shape[-1]), x.dtype)
            hn, hs = jax.lax.scan(step, h0, (a.transpose(1, 0, 2), nx.transpose(1, 0, 2)))
            h_seq = hs.transpose(1, 0, 2)
            out = jnp.einsum('btl,ld->btd', h_seq * y, w_out) + b_out
            return (out, hn)
        key = jax.random.key(seed)
        ks = jax.random.split(key, 12)
        s = 0.02
        f32 = jnp.float32
        return {'x': jax.random.normal(ks[0], (B, T, D), f32), 'w_y': jax.random.normal(ks[1], (D, L), f32) * s, 'b_y': jnp.zeros((L,), f32), 'w_x': jax.random.normal(ks[2], (D, L), f32) * s, 'b_x': jnp.zeros((L,), f32), 'conv_w': jax.random.normal(ks[3], (K, L), f32) * s, 'conv_b': jnp.zeros((L,), f32), 'a_param': jax.random.uniform(ks[4], (L,), f32, 0.5, 4.0), 'w_ig': jax.random.normal(ks[5], (L, L), f32) * s, 'b_ig': jnp.zeros((L,), f32), 'w_ag': jax.random.normal(ks[6], (L, L), f32) * s, 'b_ag': jnp.zeros((L,), f32), 'w_out': jax.random.normal(ks[7], (L, D), f32) * s, 'b_out': jnp.zeros((D,), f32)}
    _L1_attn_in = _L1_attn_setup()

    def _L1_ffn_setup():
        import jax, jax.numpy as jnp
        import numpy as np
        ZERO_POINT = 128.0

        def _dequant(wq, scale):
            return (wq.astype(jnp.float32) - ZERO_POINT) * scale[:, None]
        key = jax.random.key(seed)
        ks = jax.random.split(key, 7)
        H, I = (512, 2048)
        B, S = (2, 512)
        hidden_state = jax.random.normal(ks[0], (B, S, H), dtype=jnp.float32)
        gate_w = jax.random.randint(ks[1], (I, H), 0, 64, dtype=jnp.int32)
        up_w = jax.random.randint(ks[2], (I, H), 0, 64, dtype=jnp.int32)
        down_w = jax.random.randint(ks[3], (H, I), 0, 64, dtype=jnp.int32)
        gate_scale = jax.random.uniform(ks[4], (I,), dtype=jnp.float32) * 0.02
        up_scale = jax.random.uniform(ks[5], (I,), dtype=jnp.float32) * 0.02
        down_scale = jax.random.uniform(ks[6], (H,), dtype=jnp.float32) * 0.02
        return {'hidden_state': hidden_state, 'gate_w': gate_w, 'gate_scale': gate_scale, 'up_w': up_w, 'up_scale': up_scale, 'down_w': down_w, 'down_scale': down_scale}
    _L1_ffn_in = _L1_ffn_setup()
    _d = {'L0_attn_hidden_states': _L0_attn_in['hidden_states'], 'L0_attn_W_in': _L0_attn_in['W_in'], 'L0_attn_conv_w': _L0_attn_in['conv_w'], 'L0_attn_conv_b': _L0_attn_in['conv_b'], 'L0_attn_A_log': _L0_attn_in['A_log'], 'L0_attn_D_skip': _L0_attn_in['D_skip'], 'L0_attn_dt_bias': _L0_attn_in['dt_bias'], 'L0_attn_norm_w': _L0_attn_in['norm_w'], 'L0_attn_W_out': _L0_attn_in['W_out'], 'L0_ffn_weight': _L0_ffn_in['weight'], 'L0_ffn_scale': _L0_ffn_in['scale'], 'L1_attn_w_y': _L1_attn_in['w_y'], 'L1_attn_b_y': _L1_attn_in['b_y'], 'L1_attn_w_x': _L1_attn_in['w_x'], 'L1_attn_b_x': _L1_attn_in['b_x'], 'L1_attn_conv_w': _L1_attn_in['conv_w'], 'L1_attn_conv_b': _L1_attn_in['conv_b'], 'L1_attn_a_param': _L1_attn_in['a_param'], 'L1_attn_w_ig': _L1_attn_in['w_ig'], 'L1_attn_b_ig': _L1_attn_in['b_ig'], 'L1_attn_w_ag': _L1_attn_in['w_ag'], 'L1_attn_b_ag': _L1_attn_in['b_ag'], 'L1_attn_w_out': _L1_attn_in['w_out'], 'L1_attn_b_out': _L1_attn_in['b_out'], 'L1_ffn_gate_w': _L1_ffn_in['gate_w'], 'L1_ffn_gate_scale': _L1_ffn_in['gate_scale'], 'L1_ffn_up_w': _L1_ffn_in['up_w'], 'L1_ffn_up_scale': _L1_ffn_in['up_scale'], 'L1_ffn_down_w': _L1_ffn_in['down_w'], 'L1_ffn_down_scale': _L1_ffn_in['down_scale']}
    _x0 = _d['L0_attn_hidden_states']
    _d['L0_attn_hidden_states'] = jax.random.normal(jax.random.fold_in(jax.random.key(seed), 1), (2, 1024, 512), dtype=_x0.dtype)
    del _x0
    return _d

def reference(L0_attn_hidden_states, L0_attn_W_in, L0_attn_conv_w, L0_attn_conv_b, L0_attn_A_log, L0_attn_D_skip, L0_attn_dt_bias, L0_attn_norm_w, L0_attn_W_out, L0_ffn_weight, L0_ffn_scale, L1_attn_w_y, L1_attn_b_y, L1_attn_w_x, L1_attn_b_x, L1_attn_conv_w, L1_attn_conv_b, L1_attn_a_param, L1_attn_w_ig, L1_attn_b_ig, L1_attn_w_ag, L1_attn_b_ag, L1_attn_w_out, L1_attn_b_out, L1_ffn_gate_w, L1_ffn_gate_scale, L1_ffn_up_w, L1_ffn_up_scale, L1_ffn_down_w, L1_ffn_down_scale):

    def _L0_attn_ref(hidden_states, W_in, conv_w, conv_b, A_log, D_skip, dt_bias, norm_w, W_out):
        import jax, jax.numpy as jnp
        import numpy as np
        D_MODEL = 512
        D_STATE = 16
        D_CONV = 4
        EXPAND = 2
        D_INNER = EXPAND * D_MODEL
        HEAD_DIM = 64
        N_HEADS = D_INNER // HEAD_DIM
        N_GROUPS = 1
        CONV_DIM = D_INNER + 2 * N_GROUPS * D_STATE
        IN_DIM = D_INNER + CONV_DIM + N_HEADS
        BATCH, SEQ = (2, 1024)
        EPS = 1e-05
        b, l, _ = hidden_states.shape
        zxbcdt = jnp.einsum('bld,di->bli', hidden_states, W_in)
        gate = zxbcdt[..., :D_INNER]
        xBC = zxbcdt[..., D_INNER:D_INNER + CONV_DIM]
        dt = zxbcdt[..., D_INNER + CONV_DIM:]
        xpad = jnp.pad(xBC, ((0, 0), (D_CONV - 1, 0), (0, 0)))
        conv = conv_b
        for k in range(D_CONV):
            conv = conv + xpad[:, k:k + l, :] * conv_w[:, k]
        xBC = jax.nn.silu(conv)
        x = xBC[..., :D_INNER].reshape(b, l, N_HEADS, HEAD_DIM)
        Bm = xBC[..., D_INNER:D_INNER + D_STATE]
        Cm = xBC[..., D_INNER + D_STATE:]
        dt = jax.nn.softplus(dt + dt_bias)
        A = -jnp.exp(A_log)
        dA = jnp.exp(dt * A)
        xs = x.transpose(1, 0, 2, 3)
        Bs = Bm.transpose(1, 0, 2)
        Cs = Cm.transpose(1, 0, 2)
        dts = dt.transpose(1, 0, 2)
        dAs = dA.transpose(1, 0, 2)
        h0 = jnp.zeros((b, N_HEADS, HEAD_DIM, D_STATE), hidden_states.dtype)

        def step(h, inp):
            x_t, B_t, C_t, dt_t, dA_t = inp
            h = h * dA_t[:, :, None, None] + (dt_t[:, :, None] * x_t)[..., None] * B_t[:, None, None, :]
            y = jnp.einsum('bhpn,bn->bhp', h, C_t)
            return (h, y)
        _, ys = jax.lax.scan(step, h0, (xs, Bs, Cs, dts, dAs))
        y = ys.transpose(1, 0, 2, 3) + D_skip[None, None, :, None] * x
        y = y.reshape(b, l, D_INNER)
        y = y * jax.nn.silu(gate)
        var = jnp.mean(y * y, axis=-1, keepdims=True)
        y = y * jax.lax.rsqrt(var + EPS) * norm_w
        return jnp.einsum('bld,do->blo', y, W_out)

    def _L0_ffn_ref(x, weight, scale):
        import jax, jax.numpy as jnp
        import numpy as np
        EPS = 1e-07
        CURVATURE = 1.0
        MAX_NORM_RATIO = 0.99
        B, L, N, K = (4, 512, 512, 512)

        def _ternary_init(key, n, k):
            rand = jax.random.normal(key, (n, k), dtype=jnp.float32)
            threshold = 0.5 * jnp.mean(jnp.abs(rand))
            return jnp.where(rand > threshold, 1.0, jnp.where(rand < -threshold, -1.0, 0.0)).astype(jnp.float32)
        sqrt_c = jnp.sqrt(jnp.float32(CURVATURE))
        out = jnp.einsum('bln,nk->blk', x, weight) * scale
        v_norm = jnp.maximum(jnp.linalg.norm(out, axis=-1, keepdims=True), EPS)
        scaled_norm = sqrt_c * v_norm
        out = out * (jnp.tanh(scaled_norm) / (scaled_norm + EPS))
        max_norm = MAX_NORM_RATIO / sqrt_c
        o_norm = jnp.maximum(jnp.linalg.norm(out, axis=-1, keepdims=True), EPS)
        out = out * jnp.minimum(max_norm / o_norm, 1.0)
        return out.astype(x.dtype)

    def _L1_attn_ref(x, w_y, b_y, w_x, b_x, conv_w, conv_b, a_param, w_ig, b_ig, w_ag, b_ag, w_out, b_out):
        import jax, jax.numpy as jnp
        import numpy as np
        B, T, D, L, K = (4, 512, 512, 512, 4)

        def _reference_tuple_inner(x, w_y, b_y, w_x, b_x, conv_w, conv_b, a_param, w_ig, b_ig, w_ag, b_ag, w_out, b_out):
            Tn = x.shape[1]
            y = jax.nn.gelu(jnp.einsum('btd,dl->btl', x, w_y) + b_y, approximate=False)
            xb = jnp.einsum('btd,dl->btl', x, w_x) + b_x
            xp = jnp.pad(xb, ((0, 0), (K - 1, 0), (0, 0)))
            conv = conv_b
            for k in range(K):
                conv = conv + conv_w[k] * xp[:, k:k + Tn]
            gate_x = jax.nn.sigmoid(jnp.einsum('btl,lm->btm', conv, w_ig) + b_ig)
            gate_a = jax.nn.sigmoid(jnp.einsum('btl,lm->btm', conv, w_ag) + b_ag)
            log_a = -8.0 * gate_a * jax.nn.softplus(a_param)
            a = jnp.exp(log_a)
            mult = jnp.sqrt(1.0 - jnp.exp(2.0 * log_a))
            reset = (jnp.arange(Tn) == 0)[None, :, None]
            a = jnp.where(reset, 0.0, a)
            mult = jnp.where(reset, 1.0, mult)
            nx = gate_x * conv * mult

            def step(h, inp):
                a_t, x_t = inp
                h = a_t * h + x_t
                return (h, h)
            h0 = jnp.zeros((x.shape[0], a.shape[-1]), x.dtype)
            hn, hs = jax.lax.scan(step, h0, (a.transpose(1, 0, 2), nx.transpose(1, 0, 2)))
            h_seq = hs.transpose(1, 0, 2)
            out = jnp.einsum('btl,ld->btd', h_seq * y, w_out) + b_out
            return (out, hn)
        return _reference_tuple_inner(x, w_y, b_y, w_x, b_x, conv_w, conv_b, a_param, w_ig, b_ig, w_ag, b_ag, w_out, b_out)[0]

    def _L1_ffn_ref(hidden_state, gate_w, gate_scale, up_w, up_scale, down_w, down_scale):
        import jax, jax.numpy as jnp
        import numpy as np
        ZERO_POINT = 128.0

        def _dequant(wq, scale):
            return (wq.astype(jnp.float32) - ZERO_POINT) * scale[:, None]
        Wg = _dequant(gate_w, gate_scale)
        Wu = _dequant(up_w, up_scale)
        Wd = _dequant(down_w, down_scale)
        g = jnp.einsum('bsh,ih->bsi', hidden_state, Wg)
        u = jnp.einsum('bsh,ih->bsi', hidden_state, Wu)
        h = jax.nn.silu(g) * u
        return jnp.einsum('bsi,hi->bsh', h, Wd)
    x = L0_attn_hidden_states
    x = _layernorm(x + _L0_attn_ref(x, L0_attn_W_in, L0_attn_conv_w, L0_attn_conv_b, L0_attn_A_log, L0_attn_D_skip, L0_attn_dt_bias, L0_attn_norm_w, L0_attn_W_out), axis=-1)
    x = _layernorm(x + _L0_ffn_ref(x, L0_ffn_weight, L0_ffn_scale), axis=-1)
    x = _layernorm(x + _L1_attn_ref(x, L1_attn_w_y, L1_attn_b_y, L1_attn_w_x, L1_attn_b_x, L1_attn_conv_w, L1_attn_conv_b, L1_attn_a_param, L1_attn_w_ig, L1_attn_b_ig, L1_attn_w_ag, L1_attn_b_ag, L1_attn_w_out, L1_attn_b_out), axis=-1)
    x = _layernorm(x + _L1_ffn_ref(x, L1_ffn_gate_w, L1_ffn_gate_scale, L1_ffn_up_w, L1_ffn_up_scale, L1_ffn_down_w, L1_ffn_down_scale), axis=-1)
    return x

_drawn_inputs = setup_inputs


def setup_inputs(seed=0):
    import zlib

    import numpy as np

    out = dict(_drawn_inputs(seed))
    spreads = {'L0_attn_conv_b': (0.0, 0.1),
     'L0_attn_D_skip': (1.0, 0.2),
     'L0_attn_dt_bias': (1.0, 0.6),
     'L0_attn_norm_w': (1.0, 0.2),
     'L0_ffn_scale': (0.04419417306780815, 0.6),
     'L1_attn_b_y': (0.0, 0.8),
     'L1_attn_b_x': (0.0, 0.8),
     'L1_attn_conv_b': (0.0, 0.677),
     'L1_attn_b_ig': (0.0, 0.8),
     'L1_attn_b_ag': (0.0, 0.8),
     'L1_attn_b_out': (0.0, 0.1)}
    factors = {'L0_attn_A_log': 64.0,
     'L1_attn_w_y': 4.761,
     'L1_attn_w_x': 8.0,
     'L1_attn_conv_w': 8.0,
     'L1_attn_a_param': 8.0,
     'L1_attn_w_ig': 8.0,
     'L1_attn_w_ag': 8.0,
     'L1_attn_w_out': 4.748}
    for name, (base, spread) in spreads.items():
        noise = np.random.default_rng([zlib.crc32(name.encode()), seed]).standard_normal(out[name].shape)
        drawn = base * np.exp(spread * noise) if base else spread * noise
        out[name] = jnp.asarray(drawn.astype(out[name].dtype))
    for name, factor in factors.items():
        out[name] = (out[name] * factor).astype(out[name].dtype)
    return out
```

```python
from contextlib import ExitStack

import concourse.bass as bass
from concourse import mybir

P = 128
D = 512
KD = D // P
F32 = mybir.dt.float32
F32R = mybir.dt.float32r
I32 = mybir.dt.int32
ACT = mybir.ActivationFunctionType
ALU = mybir.AluOpType
EPS = 1e-5
SBUF_START = 16512
SBUF_END = 229344


class Sbuf:

    def __init__(self, nc, start, end):
        self.nc, self.at, self.end = nc, start, end

    def __call__(self, name, shape, dtype):
        size = 2 if dtype == mybir.dt.bfloat16 else 4
        for n in shape[1:]:
            size *= n
        size = (size + 7) // 8 * 8
        assert self.at + size <= self.end, (name, self.at + size - self.end)
        t = self.nc.alloc_sbuf_tensor_at(name, shape, dtype, offset=self.at, align_bytes=8)
        self.at += size
        return t[:]


class Signals:

    def __init__(self, nc):
        self.nc, self.taken = nc, []

    def __call__(self, name):
        self.taken.append(self.nc.alloc_semaphore(name=name))
        return self.taken[-1]

    def reset(self):
        self.nc.clear_and_free_semaphores(self.taken)
        self.nc.all_engine_barrier()
        self.taken = []


def chain(eng, sem, base):
    count = [0]

    def link(ins):
        count[0] += 1
        ins.then_inc(sem, 1)
        eng.wait_ge(sem, base + count[0])

    return link


def wait(eng, sem, value):
    if not isinstance(value, int) or value > 0:
        eng.wait_ge(sem, value)


def tiles(eng, n, step):
    step(0)
    if n > 1:
        with eng.Fori(1, n) as t:
            step(t)
def mamba2(nc, signals, x_in, x_out, w_x, w_bc, w_gate, w_out, conv, a_log, dt_bias, d_skip, norm_w, fill):
    T = 256
    B = 2
    C = T // P
    NT = x_in.shape[0] // (B * C)
    NS = NT * B
    DI = w_x.shape[1]
    M = DI // P
    H = a_log.shape[0]
    HD = DI // H
    N = 16
    HG = P // N
    G = H // HG
    GW = DI // G
    Q = 4
    HQ = H // Q
    LIMIT = 80.0
    with ExitStack() as ctx:
        def ps(name, shape):
            return ctx.enter_context(nc.psum_tensor(name, shape, F32))[:]

        def sem(name):
            return signals("a_" + name)

        sb = Sbuf(nc, SBUF_START, SBUF_END)
        ident = sb("a_ident", [P, P], F32)
        identr = sb("a_identr", [H, H], F32R)
        spread_h = sb("a_spread_h", [H, G, HG, N], F32)
        spread_n = sb("a_spread_n", [N, HG, N], F32)
        ident4 = sb("a_ident4", [P, HQ, P], mybir.dt.bfloat16)
        mask = sb("a_mask", [P, GW], mybir.dt.bfloat16)
        zeros = sb("a_zeros", [P, P], F32)
        cvec = sb("a_cvec", [P, M + 1, 5], F32)
        nega = sb("a_nega", [H, 1], F32)
        dtb = sb("a_dtb", [H, 1], F32)
        dsk = sb("a_dsk", [P, H], F32)
        nrm = sb("a_nrm", [P, M], F32)
        powers = sb("a_powers", [P, 2], F32)
        hold = sb("a_hold", [P, 1], F32)
        stats = sb("a_stats", [P, C, 6], F32)
        mv = sb("a_mv", [P, C, 4], F32)
        ssq = sb("a_ssq", [P, C, 2], F32)
        et = sb("a_et", [P, B, G, C], F32)
        carry = sb("a_carry", [P, B, M + 1, 3], F32)
        zero3 = sb("a_zero3", [P, 3], F32)
        wx = (sb("a_wxh", [P, KD, DI], F32R), sb("a_wxl", [P, KD, DI], F32R))
        wb = (sb("a_wbh", [P, KD, P], F32R), sb("a_wbl", [P, KD, P], F32R))
        wg = (sb("a_wgh", [P, KD, DI], F32R), sb("a_wgl", [P, KD, DI], F32R))
        wo = (sb("a_woh", [P, M, D], F32R), sb("a_wol", [P, M, D], F32R))
        xth = sb("a_xth", [P, B, KD, T], F32R)
        xtl = sb("a_xtl", [P, B, KD, T], F32R)
        dah = sb("a_dah", [H, B, T], F32R)
        dal = sb("a_dal", [H, B, T], F32R)
        ygh = sb("a_ygh", [P, M, P], F32R)
        ygl = sb("a_ygl", [P, M, P], F32R)
        at_work = sb.at
        xf = sb("a_xf", [P, C, D], F32)
        xr = sb("a_xr", [P, C, D], F32)
        pb = sb("a_pb", [64, T + 3], F32)
        xpre = sb("a_xpre", [P, 2, T + 3], F32)
        xs = sb("a_xs", [P, 2, T], F32)
        xtok = sb("a_xtok", [P, B, C, DI], F32)
        xdt = sb("a_xdt", [P, DI], F32)
        sg = sb("a_sg", [P, DI], F32)
        L = sb("a_L", [P, H, P], F32)
        yg = sb("a_yg", [P, DI], F32)
        S = sb("a_S", [P, B, G, GW], F32)
        bcs = sb("a_bcs", [P, B, T], F32)
        cs = sb("a_cs", [N, B, T], F32)
        ex = sb("a_ex", [P, B, G, T], F32)
        tmp = sb("a_tmp", [P, GW], F32)
        btok = sb("a_btok", [P, C, P], F32)
        gs = sb("a_gs", [P, P], F32)
        bw = sb("a_bw", [P, H, N], F32)
        z = sb("a_z", [H, T], F32)
        e = sb("a_e", [H, T], F32)
        u = sb("a_u", [H, T], F32)
        l = sb("a_l", [H, T], F32)
        one = sb("a_one", [H, T], mybir.dt.bfloat16)
        stage = Sbuf(nc, at_work, sb.at)("a_stage", [P, 4, 2 * D], F32)

        ps_t = ps("a_pst", [P, 2, KD, P])
        ps_r = ps("a_psr", [P, 2, D])
        ps_m = ps("a_psm", [P, D])
        ps_d = ps("a_psd", [P, HQ, P])
        ps_y = ps("a_psy", [P, G, GW])

        s_small, s_const, s_prep = sem("small"), sem("const"), sem("prep")
        s_stage = [sem(f"stage{i}") for i in range(4)]
        s_whi, s_wlo = sem("whi"), sem("wlo")
        s_x = [sem(f"x{j}") for j in range(C)]
        s_xr = [sem(f"xr{j}") for j in range(C)]
        s_st = [sem(f"st{j}") for j in range(C)]
        s_xt, s_xh, s_xl = sem("xt"), sem("xh"), sem("xl")
        s_bp, s_mb, s_bedge, s_bkeep, s_bacc, s_bchain, s_bc = (sem(n) for n in ("bp", "mb", "bedge", "bkeep", "bacc", "bchain", "bc"))
        s_bs, s_cs, s_bchain2 = sem("bs"), sem("cs"), sem("bchain2")
        s_dt, s_dta, s_dtr, s_dah, s_dal = sem("dt"), sem("dta"), sem("dtr"), sem("dah"), sem("dal")
        s_xp, s_pre, s_acc, s_edge, s_keep, s_xchain, s_xc, s_xs, s_xtr, s_xtok = (
            sem(n) for n in ("xp", "pre", "acc", "edge", "keep", "xchain", "xc", "xs", "xtr", "xtok"))
        s_gp, s_gs, s_dp, s_sc, s_bw, s_m, s_gate, s_sg = (sem(n) for n in ("gp", "gs", "dp", "sc", "bw", "m", "gate", "sg"))
        s_xdt, s_dx, s_yp, s_stp, s_stm, s_su, s_ga, s_yg, s_sq, s_rs = (
            sem(n) for n in ("xdt", "dx", "yp", "stp", "stm", "su", "ga", "yg", "sq", "rs"))
        s_yt, s_yh, s_yl, s_op, s_res, s_var, s_std, s_ln, s_ze, s_oe, s_bn = (
            sem(n) for n in ("yt", "yh", "yl", "op", "res", "var", "std", "ln", "ze", "oe", "bn"))
        s_dr, s_ec, s_et, s_cr, s_cx, s_btp, s_bt = (sem(n) for n in ("dr", "ec", "et", "cr", "cx", "btp", "bt"))

        pieces = [(w_bc.rearrange("(k p) n -> p k n", p=P), wb[0], wb[1], KD, None)]
        for w_dram, w in ((w_x, wx), (w_gate, wg)):
            for k in range(KD):
                pieces.append((w_dram[k * P:(k + 1) * P, :], w[0][:, k, :], w[1][:, k, :], 1, None))
        n_gate = len(pieces)
        for m in range(0, M, 2):
            pieces.append((w_out[m * P:(m + 2) * P, :].rearrange("(a p) n -> p a n", p=P), wo[0][:, m:m + 2, :], wo[1][:, m:m + 2, :], 2, m))

        def staged(i):
            w, a = pieces[i][1], pieces[i][3]
            if a == 1:
                return stage[:, i % 4, :]
            return stage[:, i % 4, 0:a * w.shape[2]].rearrange("p (a n) -> p a n", a=a)

        def chunk(dram, t, b, j):
            return dram[bass.ds(t * C + (b * NT * C + j), 1), :, :].rearrange("a p d -> p (a d)")

        def nothing(*_):
            pass

        def before(t, b, n=1):
            b -= n
            while b < 0:
                t, b = t - 1, b + B
            return t, b

        def steps(eng, turn=nothing, lead=nothing, front=nothing, ssm=nothing, soft=nothing, rest=nothing, x_part=nothing,
                  z_part=nothing, o_part=nothing):
            def step(t, b):
                prev = before(t, b)
                has_prev = not isinstance(t, int) or t * B + b > 0
                turn(t, b)
                if has_prev:
                    lead(*prev, 0)
                front(t, b)
                if has_prev:
                    ssm(*prev, 0, lambda i: soft(t, b, 0) if i == 0 else None)
                else:
                    soft(t, b, 0)
                x_part(t, b, 0, lambda: [lead(*prev, 1) if has_prev else None, soft(t, b, 1)])
                if has_prev:
                    z_part(*prev, 0)
                    ssm(*prev, 1, lambda i: soft(t, b, 2 + i))
                else:
                    soft(t, b, 2)
                    soft(t, b, 3)
                x_part(t, b, 1, (lambda: [o_part(*prev, 0, i) for i in range(3)]) if has_prev else nothing)
                if has_prev:
                    z_part(*prev, 1)
                rest(t, b, (lambda i: o_part(*prev, 1, i)) if has_prev else nothing)

            for b in range(B):
                step(0, b)
            with eng.Fori(1, NT) as t:
                for b in range(B):
                    step(t, b)
            end = (NT - 1, B - 1)
            for j in range(C):
                lead(*end, j)
                ssm(*end, j, nothing)
                z_part(*end, j)
                for i in range(3):
                    o_part(*end, j, i)

        block = ctx.enter_context(nc.Block())

        @block.sync
        def _(sp):
            for dst, src in ((cvec, conv), (nega, a_log.rearrange("(h a) -> h a", a=1)), (dtb, dt_bias.rearrange("(h a) -> h a", a=1)),
                             (dsk, d_skip.partition_broadcast(P)), (nrm, norm_w)):
                sp.dma_start(dst, src).then_inc(s_small, 16)
            for i, piece in enumerate(pieces):
                if i >= 4:
                    sp.wait_ge(s_wlo, i - 3)
                sp.dma_start(staged(i), piece[0]).then_inc(s_stage[i % 4], 16)
            sp.wait_ge(s_wlo, len(pieces))

            def store(t, b):
                s = B * t + b
                for j in range(C):
                    sp.wait_ge(s_ln, C * s + j + 1)
                    sp.dma_start(chunk(x_out, t, b, j), xr[:, j, :]).then_inc(s_st[j], 16)

            def load_r(t, b):
                s = B * t + b
                for j in range(C):
                    wait(sp, s_st[j], 16 * s)
                    sp.dma_start(xr[:, j, :], chunk(x_in, t, b, j)).then_inc(s_xr[j], 16)

            def step(t, b):
                s = B * t + b
                for j in range(C):
                    wait(sp, s_xt, C * (s - 1) + j + 1)
                    sp.dma_start(xf[:, j, :], chunk(x_in, t, b, j)).then_inc(s_x[j], 16)
                if not isinstance(t, int) or s > 1:
                    store(*before(t, b, 2))
                if not isinstance(t, int) or s > 0:
                    load_r(*before(t, b))

            for b in range(B):
                step(0, b)
            with sp.Fori(1, NT) as t:
                for b in range(B):
                    step(t, b)
            store(NT - 1, 0)
            load_r(NT - 1, 1)
            store(NT - 1, 1)
            for j in range(C):
                sp.wait_ge(s_st[j], 16 * NS)

        @block.gpsimd
        def _(pool):
            fill(pool, ident, s_const)
            pool.memset(powers[:, 0:1], EPS)
            pool.memset(powers[:, 1:2], -0.5).then_inc(s_const, 1)
            pool.memset(zero3, 0.0).then_inc(s_const, 1)
            pool.memset(zeros, 0.0).then_inc(s_const, 1)
            pool.wait_ge(s_const, 5)
            for h in range(HQ):
                pool.tensor_copy(ident4[:, h, :], ident).then_inc(s_const, 1)
            pool.tensor_copy(identr, ident[0:H, 0:H]).then_inc(s_const, 1)
            for g in range(G):
                pool.tensor_copy(spread_h[:, g], ident[0:H, g * HG:(g + 1) * HG].unsqueeze(2).broadcast_to([H, HG, N])).then_inc(s_const, 1)
            pool.tensor_copy(spread_n, ident[0:N, 0:N].unsqueeze(1).broadcast_to([N, HG, N])).then_inc(s_const, 1)
            heads = mask.rearrange("r (h p) -> r h p", h=HG)
            pool.memset(mask, 1.0).then_inc(s_const, 1)
            pool.wait_ge(s_const, 10 + HQ)
            pool.affine_select(out=heads, in_=heads, compare_op=ALU.is_ge, fill=0.0, base=0,
                               pattern=[[-N, HG], [0, HD]], channel_multiplier=1).then_inc(s_const, 1)
            pool.wait_ge(s_const, 11 + HQ)
            pool.affine_select(out=heads, in_=heads, compare_op=ALU.is_ge, fill=0.0, base=N - 1,
                               pattern=[[N, HG], [0, HD]], channel_multiplier=-1).then_inc(s_const, 1)
            pool.wait_ge(s_wlo, len(pieces))
            pool.memset(S, 0.0).then_inc(s_const, 1)
            pool.memset(bcs, 0.0).then_inc(s_const, 1)
            pool.wait_ge(s_small, 80)
            pool.wait_ge(s_const, 14 + HQ)

            def front(t, b):
                s = B * t + b
                wait(pool, s_bc, s)
                wait(pool, s_bkeep, s)
                if isinstance(t, int):
                    pool.memset(pb[:, 0:3], 0.0).then_inc(s_bedge, 1)
                else:
                    pool.tensor_tensor(pb[:, 0:3], carry[0:64, b, M], zero3[0:64], ALU.add).then_inc(s_bedge, 1)
                pool.wait_ge(s_bedge, s + 1)
                pool.wait_ge(s_mb, 2 * s + 1)
                pool.tensor_tensor(carry[0:64, b, M], pb[:, T:T + 3], zero3[0:64], ALU.add).then_inc(s_bkeep, 1)

            def x_part(t, b, half, fill):
                s = B * t + b
                for m in range(4 * half, 4 * half + 4):
                    n = M * s + m
                    wait(pool, s_xc, n - 1)
                    wait(pool, s_keep, n)
                    if isinstance(t, int):
                        pool.memset(xpre[:, m % 2, 0:3], 0.0).then_inc(s_edge, 1)
                    else:
                        pool.tensor_tensor(xpre[:, m % 2, 0:3], carry[:, b, m], zero3, ALU.add).then_inc(s_edge, 1)
                    pool.wait_ge(s_edge, n + 1)
                    pool.wait_ge(s_pre, n + 1)
                    pool.tensor_tensor(carry[:, b, m], xpre[:, m % 2, T:T + 3], zero3, ALU.add).then_inc(s_keep, 1)
                fill()

            def ssm(t, b, j, between):
                n = C * (B * t + b) + j
                pool.wait_ge(s_xdt, n + 1)
                xj = xtok[:, b, j, :].rearrange("p (h d) -> p h d", h=H)
                pool.tensor_tensor(xj, xj, dsk.unsqueeze(2).broadcast_to([P, H, HD]), ALU.mult).then_inc(s_dx, 1)

            def root(v, out, eps_added, done, n):
                pool.tensor_tensor(v, v, powers[:, 0:1], ALU.add).then_inc(eps_added, 1)
                pool.wait_ge(eps_added, n + 1)
                pool.tensor_tensor(out, v, powers[:, 1:2], ALU.pow).then_inc(done, 1)

            def z_part(t, b, j):
                n = C * (B * t + b) + j
                pool.wait_ge(s_sq, n + 1)
                root(ssq[:, j, 0:1], ssq[:, j, 1:2], s_ze, s_rs, n)

            def o_part(t, b, j, third):
                if third == 0:
                    n = C * (B * t + b) + j
                    pool.wait_ge(s_var, n + 1)
                    root(mv[:, j, 1:2], mv[:, j, 2:3], s_oe, s_std, n)

            def rest(t, b, fill):
                fill(0)

            steps(pool, front=front, ssm=ssm, rest=rest, x_part=x_part, z_part=z_part, o_part=o_part)

        @block.scalar
        def _(act):
            act.wait_ge(s_small, 80)
            for i, (_, hi, _, _, m) in enumerate(pieces):
                act.wait_ge(s_stage[i % 4], 16 * (i // 4 + 1))
                if m is None:
                    act.activation(hi, staged(i), ACT.Copy).then_inc(s_whi, 1)
                else:
                    act.activation(hi[:, 0, :], staged(i)[:, 0, :], ACT.Copy, scale=nrm[:, m:m + 1])
                    act.activation(hi[:, 1, :], staged(i)[:, 1, :], ACT.Copy, scale=nrm[:, m + 1:m + 2]).then_inc(s_whi, 1)
            act.wait_ge(s_prep, 1)
            act.activation(nega, nega, ACT.Exp).then_inc(s_prep, 1)
            act.wait_ge(s_prep, 3)
            act.wait_ge(s_const, 14 + HQ)
            act.wait_ge(s_wlo, len(pieces))

            def turn(t, b):
                s = B * t + b
                for j in range(C):
                    act.wait_ge(s_xt, C * s + j + 1)
                    act.activation(xth[:, b, :, j * P:(j + 1) * P], ps_t[:, j, :, :], ACT.Copy).then_inc(s_xh, 1)

            def lead(t, b, j):
                n = C * (B * t + b) + j
                act.wait_ge(s_gp, n + 1)
                wait(act, s_m, Q * n)
                act.activation(gs, ps_m[:, 0:P], ACT.Copy).then_inc(s_gs, 1)

            def front(t, b):
                s = B * t + b
                act.wait_ge(s_bp, s + 1)
                wait(act, s_bc, s)
                wait(act, s_bkeep, s)
                act.activation(pb[:, 3:T + 3], ps_m[0:64, 0:T], ACT.Copy).then_inc(s_mb, 1)
                act.activation(z, ps_m[64:64 + H, 0:T], ACT.Copy).then_inc(s_mb, 1)
                act.wait_ge(s_mb, 2 * s + 1)
                act.activation(bcs[0:64, b, :], pb[:, 3:T + 3], ACT.Identity, bias=cvec[0:64, M, 4:5],
                               scale=cvec[0:64, M, 3:4]).then_inc(s_bacc, 1)

            def soft(t, b, part):
                s = B * t + b
                if part == 0:
                    act.wait_ge(s_dt, 9 * s + 2)
                    act.activation(e, e, ACT.Exp).then_inc(s_dta, 1)
                    act.wait_ge(s_dt, 9 * s + 3)
                    act.activation(l, u, ACT.Ln).then_inc(s_dta, 1)
                if part == 2:
                    act.wait_ge(s_dt, 9 * s + 9)
                    act.activation(bcs[64:64 + H, b, :], z, ACT.Copy).then_inc(s_dtr, 1)
                    act.activation(e, z, ACT.Exp, scale=nega).then_inc(s_dta, 1)
                    act.wait_ge(s_dta, 3 * s + 3)
                    act.activation(dah[:, b, :], e, ACT.Copy).then_inc(s_dah, 1)
                    act.wait_ge(s_bc, s + 1)
                    act.activation(bcs[0:64, b, :], bcs[0:64, b, :], ACT.Silu).then_inc(s_bs, 1)
                    act.wait_ge(s_bs, s + 1)
                    act.activation(cs[:, b, :], bcs[32:32 + N, b, :], ACT.Copy).then_inc(s_cs, 1)

            def ssm(t, b, j, between):
                n = C * (B * t + b) + j
                for g in range(G):
                    act.wait_ge(s_gate, G * n + g + 1)
                    wait(act, s_yg, G * (n - 1) + g + 1)
                    act.activation(sg[:, g * GW:(g + 1) * GW], ps_r[:, g, :], ACT.Silu).then_inc(s_sg, 1)
                between(0)

            def x_part(t, b, half, fill):
                s = B * t + b
                base = 4 * half
                for i in range(6):
                    if i < 4:
                        m = base + i
                        n = M * s + m
                        act.wait_ge(s_xp, n + 1)
                        wait(act, s_xc, n - 1)
                        wait(act, s_keep, n - 1)
                        act.activation(xpre[:, m % 2, 3:T + 3], ps_r[:, m % 2, 0:T], ACT.Copy).then_inc(s_pre, 1)
                        act.wait_ge(s_pre, n + 1)
                        wait(act, s_xtr, n - 1)
                        act.activation(xs[:, m % 2, :], xpre[:, m % 2, 3:T + 3], ACT.Identity, bias=cvec[:, m, 4:5],
                                       scale=cvec[:, m, 3:4]).then_inc(s_acc, 1)
                    if 1 <= i < 5:
                        m = base + i - 1
                        act.wait_ge(s_xc, M * s + m + 1)
                        act.activation(xs[:, m % 2, :], xs[:, m % 2, :], ACT.Silu).then_inc(s_xs, 1)
                    if i == 4:
                        fill()
                    if i >= 2:
                        m = base + i - 2
                        act.wait_ge(s_xtr, M * s + m + 1)
                        act.activation(xtok[:, b, :, m * P:(m + 1) * P], ps_t[:, m % 2, 0:C, :], ACT.Copy).then_inc(s_xtok, 1)

            def z_part(t, b, j):
                n = C * (B * t + b) + j
                act.wait_ge(s_yg, G * n + G)
                act.activation(xtok[:, b, j, :], yg, ACT.Square, scale=DI ** -0.5, accum_out=ssq[:, j, 0:1]).then_inc(s_sq, 1)
                for q in range(2):
                    act.wait_ge(s_yt, 2 * n + q + 1)
                    act.activation(ygh[:, 4 * q:4 * q + 4, :], ps_t[:, q, :, :], ACT.Copy).then_inc(s_yh, 1)

            def rest(t, b, fill):
                s = B * t + b
                act.wait_ge(s_btp, s + 1)
                wait(act, s_m, Q * C * s)
                act.activation(btok, ps_m[:, 0:C * P].rearrange("p (j n) -> p j n", j=C), ACT.Copy).then_inc(s_bt, 1)

            steps(act, turn=turn, lead=lead, front=front, ssm=ssm, soft=soft, rest=rest, x_part=x_part, z_part=z_part)

        @block.vector
        def _(dve):
            dve.wait_ge(s_small, 80)
            for i, (_, hi, lo, _, m) in enumerate(pieces):
                dve.wait_ge(s_whi, i + 1)
                if m is None:
                    dve.tensor_tensor(lo, staged(i), hi.bitcast(F32), ALU.subtract).then_inc(s_wlo, 1)
                else:
                    for a in range(2):
                        ins = dve.scalar_tensor_tensor(out=lo[:, a, :], in0=staged(i)[:, a, :], scalar=nrm[:, m + a:m + a + 1],
                                                       in1=hi[:, a, :].bitcast(F32), op0=ALU.mult, op1=ALU.subtract)
                    ins.then_inc(s_wlo, 1)
            dve.tensor_scalar(nega, nega, LIMIT, None, ALU.min).then_inc(s_prep, 1)
            dve.wait_ge(s_prep, 2)
            dve.tensor_scalar(nega, nega, -1.0, None, ALU.mult).then_inc(s_prep, 1)
            dve.wait_ge(s_const, 14 + HQ)

            def taps(dst, src, vec, link_sem, base, done):
                for k in range(3):
                    ins = dve.scalar_tensor_tensor(out=dst, in0=src[:, k:k + T], scalar=vec[:, k:k + 1], in1=dst, op0=ALU.mult, op1=ALU.add)
                    if k < 2:
                        ins.then_inc(link_sem, 1)
                        dve.wait_ge(link_sem, base + k + 1)
                ins.then_inc(done, 1)

            def turn(t, b):
                s = B * t + b
                for j in range(C):
                    dve.wait_ge(s_xh, C * s + j + 1)
                    cols = slice(j * P, (j + 1) * P)
                    dve.tensor_tensor(xtl[:, b, :, cols], ps_t[:, j, :, :], xth[:, b, :, cols].bitcast(F32), ALU.subtract).then_inc(s_xl, 1)

            def scan(n, q):
                hq = slice(q * HQ, (q + 1) * HQ)
                dve.wait_ge(s_dp, Q * n + q + 1)
                if q == 0:
                    wait(dve, s_yp, G * n)
                dve.tensor_tensor_scan(L[:, hq, :].rearrange("p h t -> p (h t)"), ps_d.rearrange("p h t -> p (h t)"),
                                       ident4.rearrange("p h t -> p (h t)"), 0.0, ALU.mult, ALU.add).then_inc(s_sc, 1)

            def lead(t, b, j):
                n = C * (B * t + b) + j
                heads = "p (h d) -> p h d"
                dve.wait_ge(s_bt, B * t + b + 1)
                dve.wait_ge(s_xtok, M * (B * t + b) + M)
                wait(dve, s_stp, G * n)
                dve.tensor_tensor(xdt.rearrange(heads, h=H), xtok[:, b, j, :].rearrange(heads, h=H),
                                  btok[:, j, 64:64 + H].unsqueeze(2).broadcast_to([P, H, HD]), ALU.mult).then_inc(s_xdt, 1)
                scan(n, 0)

            def front(t, b):
                s = B * t + b
                dve.wait_ge(s_bacc, s + 1)
                dve.wait_ge(s_bedge, s + 1)
                taps(bcs[0:64, b, :], pb, cvec[0:64, M, :], s_bchain, 2 * s, s_bc)
                link = chain(dve, s_dt, 9 * s)
                dve.wait_ge(s_mb, 2 * s + 2)
                link(dve.tensor_scalar(z, z, dtb, None, ALU.add))
                wait(dve, s_dr, s)
                wait(dve, s_dah, s)
                link(dve.scalar_tensor_tensor(out=e, in0=z, scalar=-1.0, in1=z, op0=ALU.mult, op1=ALU.min))

            def soft(t, b, part):
                s = B * t + b
                if part == 0:
                    dve.wait_ge(s_dta, 3 * s + 1)
                    dve.tensor_scalar(u, e, 1.0, None, ALU.add).then_inc(s_dt, 1)
                    dve.wait_ge(s_dt, 9 * s + 3)
                    dve.tensor_scalar(one, u, 1.0, None, ALU.is_equal).then_inc(s_dt, 1)
                if part == 1:
                    dve.wait_ge(s_dta, 3 * s + 2)
                    dve.wait_ge(s_dt, 9 * s + 4)
                    dve.scalar_tensor_tensor(out=u, in0=u, scalar=-1.0, in1=one, op0=ALU.add, op1=ALU.add).then_inc(s_dt, 1)
                    dve.wait_ge(s_dt, 9 * s + 5)
                    dve.reciprocal(u, u).then_inc(s_dt, 1)
                    dve.wait_ge(s_dt, 9 * s + 6)
                    dve.tensor_tensor(l, l, u, ALU.mult).then_inc(s_dt, 1)
                    dve.wait_ge(s_dt, 9 * s + 7)
                    dve.scalar_tensor_tensor(out=l, in0=l, scalar=1.0, in1=one, op0=ALU.mult, op1=ALU.add).then_inc(s_dt, 1)
                    dve.wait_ge(s_dt, 9 * s + 8)
                    dve.tensor_tensor(l, l, e, ALU.mult).then_inc(s_bchain2, 1)
                    dve.wait_ge(s_bchain2, s + 1)
                    dve.scalar_tensor_tensor(out=z, in0=z, scalar=0.0, in1=l, op0=ALU.max, op1=ALU.add).then_inc(s_dt, 1)
                if part == 3:
                    dve.wait_ge(s_dah, s + 1)
                    dve.tensor_tensor(dal[:, b, :], e, dah[:, b, :].bitcast(F32), ALU.subtract).then_inc(s_dal, 1)
                    dve.wait_ge(s_dal, 3 * s + 1)
                    for d in (dah, dal):
                        dve.memset(d.bitcast(F32)[:, b, :].rearrange("h (j n) -> h j n", j=C)[:, :, 0:1], 0.0).then_inc(s_dal, 1)

            def ssm(t, b, j, between):
                n = C * (B * t + b) + j
                for q in range(Q):
                    hq = slice(q * HQ, (q + 1) * HQ)
                    if q:
                        scan(n, q)
                    dve.wait_ge(s_sc, Q * n + q + 1)
                    dve.tensor_tensor(bw[:, hq, :], btok[:, j, 0:N].unsqueeze(1).broadcast_to([P, HQ, N]),
                                      L[:, hq, P - 1:P].broadcast_to([P, HQ, N]), ALU.mult).then_inc(s_bw, 1)
                    if q == 0:
                        dve.wait_ge(s_gs, n + 1)
                    dve.wait_ge(s_bw, Q * n + q + 1)
                    dve.tensor_tensor(L[:, hq, :], L[:, hq, :], gs.unsqueeze(1).broadcast_to([P, HQ, P]), ALU.mult).then_inc(s_m, 1)
                between(0)
                for g in range(G):
                    cols = slice(g * GW, (g + 1) * GW)
                    dve.wait_ge(s_stp, G * n + g + 1)
                    wait(dve, s_su, G * n + g)
                    dve.tensor_tensor(tmp, ps_m, mask, ALU.mult).then_inc(s_stm, 1)
                    dve.wait_ge(s_stm, G * n + g + 1)
                    dve.scalar_tensor_tensor(out=S[:, b, g, :], in0=S[:, b, g, :], scalar=et[:, b, g, j:j + 1], in1=tmp,
                                             op0=ALU.mult, op1=ALU.add).then_inc(s_su, 1)
                    dve.wait_ge(s_yp, G * n + g + 1)
                    dve.wait_ge(s_dx, n + 1)
                    wait(dve, s_yt, 2 * n)
                    wait(dve, s_sq, n)
                    dve.tensor_tensor(yg[:, cols], ps_y[:, g, :], xtok[:, b, j, cols], ALU.add).then_inc(s_ga, 1)
                    dve.wait_ge(s_ga, G * n + g + 1)
                    dve.wait_ge(s_sg, G * n + g + 1)
                    dve.tensor_tensor(yg[:, cols], yg[:, cols], sg[:, cols], ALU.mult).then_inc(s_yg, 1)
                    if g == 0:
                        between(1)

            def x_part(t, b, half, fill):
                s = B * t + b
                for m in range(4 * half, 4 * half + 4):
                    n = M * s + m
                    dve.wait_ge(s_edge, n + 1)
                    dve.wait_ge(s_acc, n + 1)
                    taps(xs[:, m % 2, :], xpre[:, m % 2, :], cvec[:, m, :], s_xchain, 2 * n, s_xc)
                fill()

            def z_part(t, b, j):
                n = C * (B * t + b) + j
                for q in range(2):
                    dve.wait_ge(s_yh, 2 * n + q + 1)
                    dve.tensor_tensor(ygl[:, 4 * q:4 * q + 4, :], ps_t[:, q, :, :], ygh[:, 4 * q:4 * q + 4, :].bitcast(F32),
                                      ALU.subtract).then_inc(s_yl, 1)

            def o_part(t, b, j, third):
                if third:
                    return
                s = B * t + b
                n = C * s + j
                out = xr[:, j, :]
                dve.wait_ge(s_rs, n + 1)
                dve.wait_ge(s_op, n + 1)
                dve.wait_ge(s_xr[j], 16 * s + 16)
                dve.scalar_tensor_tensor(out=out, in0=ps_r[:, 0, :], scalar=ssq[:, j, 1:2], in1=out, op0=ALU.mult, op1=ALU.add).then_inc(s_res, 1)
                dve.wait_ge(s_res, n + 1)
                dve.bn_stats(stats[:, j, :], out).then_inc(s_bn, 1)
                dve.wait_ge(s_bn, n + 1)
                dve.memset(hold, 0.0)
                dve.bn_aggr(mv[:, j, 0:2], stats[:, j, :]).then_inc(s_var, 1)
                dve.wait_ge(s_std, n + 1)
                dve.tensor_scalar(out, out, mv[:, j, 0:1], mv[:, j, 2:3], ALU.subtract, ALU.mult).then_inc(s_ln, 1)

            def rest(t, b, fill):
                s = B * t + b
                dve.wait_ge(s_dr, s + 1)
                for g in range(G):
                    for j in range(C):
                        cols = slice(j * P, (j + 1) * P)
                        dve.tensor_tensor_scan(ex[:, b, g, cols], ps_m[:, g * T + j * P:g * T + (j + 1) * P], zeros, 1.0,
                                               ALU.mult, ALU.add).then_inc(s_ec, 1)
                dve.wait_ge(s_ec, G * C * s + G * C)
                dve.tensor_copy(et[:, b], ex[:, b].rearrange("p g (j n) -> p g j n", j=C)[:, :, :, P - 1]).then_inc(s_et, 1)
                dve.wait_ge(s_et, s + 1)
                dve.wait_ge(s_cr, s + 1)
                dve.tensor_tensor(ex[:, b], ex[:, b], ps_m[:, 0:T].unsqueeze(1).broadcast_to([P, G, T]), ALU.mult).then_inc(s_cx, 1)
                fill(0)

            steps(dve, turn=turn, lead=lead, front=front, ssm=ssm, soft=soft, rest=rest, x_part=x_part, z_part=z_part, o_part=o_part)

        @block.tensor
        def _(pe):
            pe.wait_ge(s_const, 14 + HQ)

            def three(out, lhs, rhs, n, lo=0, hi=None):
                for k in range(lo, n if hi is None else hi):
                    for a, c in ((0, 0), (0, 1), (1, 0)):
                        last = pe.matmul(out, lhs(a, k), rhs(c, k), start=(k, a, c) == (0, 0, 0), stop=(k, a) == (n - 1, 1))
                return last

            def turn(t, b):
                s = B * t + b
                for j in range(C):
                    pe.wait_ge(s_x[j], 16 * s + 16)
                    wait(pe, s_yl, 4 * s - 5 + j)
                    wait(pe, s_xtok, M * (s - 1) + 6 + j + 1)
                    for k in range(KD):
                        last = pe.transpose(ps_t[:, j, k, :], xf[:, j, k * P:(k + 1) * P], ident)
                    last.then_inc(s_xt, 1)

            def front(t, b):
                s = B * t + b
                pe.wait_ge(s_xl, C * s + C)
                wait(pe, s_bt, s)
                wait(pe, s_gs, C * (s - 1) + 1)
                x = (xth, xtl)
                three(ps_m[:, 0:T], lambda a, k: wb[a][:, k, :], lambda c, k: x[c][:, b, k, :], KD).then_inc(s_bp, 1)

            def gate(t, b, j, g, free, lo=0, hi=KD):
                if lo == 0:
                    for f in free:
                        wait(pe, *f)
                x = (xth, xtl)
                last = three(ps_r[:, g, :], lambda a, k: x[a][:, b, k, j * P:(j + 1) * P],
                             lambda c, k: wg[c][:, k, g * GW:(g + 1) * GW], KD, lo, hi)
                if hi == KD:
                    last.then_inc(s_gate, 1)

            def decays(t, b, j, q):
                s = B * t + b
                pe.wait_ge(s_dal, 3 * s + 3)
                wait(pe, s_sc, Q * (C * s + j) + q)
                for h in range(HQ):
                    row = identr[0:H, q * HQ + h:q * HQ + h + 1].broadcast_to([H, P])
                    for i, d in enumerate((dah, dal)):
                        last = pe.matmul(ps_d[:, h, :], row, d[:, b, j * P:(j + 1) * P], start=i == 0, stop=i == 1)
                last.then_inc(s_dp, 1)

            def is_end(t, b):
                return isinstance(t, int) and B * t + b == NS - 1

            def lead(t, b, j):
                s = B * t + b
                cols = slice(j * P, (j + 1) * P)
                decays(t, b, j, 0)
                pe.wait_ge(s_cs, s + 1)
                pe.wait_ge(s_bt, s + 1)
                wait(pe, s_stm, G * (C * s + j))
                pe.matmul(ps_m[:, 0:P], bcs[0:N, b, cols], cs[:, b, cols], start=True, stop=True).then_inc(s_gp, 1)
                if j == 0:
                    free = [(s_pre, M * s + 7), (s_res, C * s)]
                elif not is_end(t, b):
                    free = [(s_pre, M * s + M + 3)]
                else:
                    free = [(s_sg, 4 * s + 1), (s_res, C * s + 1)]
                gate(t, b, j, 0, free)

            def ssm(t, b, j, between):
                s = B * t + b
                n = C * s + j
                cols = slice(j * P, (j + 1) * P)
                decays(t, b, j, 1)
                if j == 0:
                    free = [(s_pre, M * s + 8)]
                elif not is_end(t, b):
                    free = [(s_pre, M * s + M + 4)]
                else:
                    free = [(s_sg, 4 * s + 2)]
                gate(t, b, j, 1, free, 0, KD // 2)
                decays(t, b, j, 2)
                gate(t, b, j, 1, free, KD // 2, KD)
                decays(t, b, j, 3)
                pe.wait_ge(s_xdt, n + 1)
                pe.wait_ge(s_cx, s + 1)
                for g in range(G):
                    gc = slice(g * GW, (g + 1) * GW)
                    wait(pe, s_ga, G * (n - 1) + g + 1)
                    wait(pe, s_su, G * (n - 1) + g + 1)
                    pe.wait_ge(s_m, Q * n + (g + 1) * Q // G)
                    pe.matmul(ps_y[:, g, :], ex[:, b, g, cols], S[:, b, g, :], start=True, stop=False)
                    for h in range(g * HG, (g + 1) * HG):
                        o = (h - g * HG) * HD
                        last = pe.matmul(ps_y[:, g, o:o + HD], L[:, h, :], xdt[:, h * HD:(h + 1) * HD], start=False,
                                         stop=h == (g + 1) * HG - 1)
                    last.then_inc(s_yp, 1)
                    if g == 0:
                        pe.wait_ge(s_gs, n + 1)
                        if j == 0 and not is_end(t, b):
                            pe.wait_ge(s_mb, 2 * s + 4)
                    else:
                        pe.wait_ge(s_stm, G * n + g)
                    pe.matmul(ps_m[:, :], bw[:, g * HG:(g + 1) * HG, :].rearrange("p h n -> p (h n)"), xdt[:, gc], start=True, stop=True).then_inc(s_stp, 1)

            def x_part(t, b, half, fill):
                s = B * t + b
                x = (xth, xtl)
                base = 4 * half
                free = {0: [(s_sg, 4 * s - 3)], 1: [(s_sg, 4 * s - 2)], 2: [(s_pre, M * s + 1)], 3: [(s_pre, M * s + 2)],
                        4: [(s_sg, 4 * s - 1), (s_pre, M * s + 3)], 5: [(s_sg, 4 * s), (s_pre, M * s + 4)],
                        6: [(s_pre, M * s + 5)], 7: [(s_pre, M * s + 6)]}
                tfree = {0: [(s_xl, C * s + 1)], 1: [(s_xl, C * s + 2)], 2: [(s_xtok, M * s + 1)], 3: [(s_xtok, M * s + 2)],
                         4: [(s_yl, 4 * s - 3), (s_xtok, M * s + 3)], 5: [(s_yl, 4 * s - 2), (s_xtok, M * s + 4)],
                         6: [(s_xtok, M * s + 5)], 7: [(s_xtok, M * s + 6)]}
                for i in range(6):
                    if i < 4:
                        m = base + i
                        for f in free[m]:
                            wait(pe, *f)
                        three(ps_r[:, m % 2, 0:T], lambda a, k: wx[a][:, k, m * P:(m + 1) * P], lambda c, k: x[c][:, b, k, :],
                              KD).then_inc(s_xp, 1)
                    if i == 4:
                        fill()
                    if i >= 2:
                        m = base + i - 2
                        pe.wait_ge(s_xs, M * s + m + 1)
                        for f in tfree[m]:
                            wait(pe, *f)
                        for j in range(C):
                            last = pe.transpose(ps_t[:, m % 2, j, :], xs[:, m % 2, j * P:(j + 1) * P], ident)
                        last.then_inc(s_xtr, 1)

            def z_part(t, b, j):
                s = B * t + b
                n = C * s + j
                for q in range(2):
                    if not is_end(t, b):
                        pe.wait_ge(s_xtok, M * (s + 1) + 4 * j + 2 + q + 1)
                    else:
                        pe.wait_ge(s_yl, 2 * (n - 1) + q + 1)
                    pe.wait_ge(s_yg, G * n + q + 1)
                    for i in range(4):
                        last = pe.transpose(ps_t[:, q, i, :], yg[:, (4 * q + i) * P:(4 * q + i + 1) * P], ident)
                    last.then_inc(s_yt, 1)

            def o_part(t, b, j, third):
                s = B * t + b
                n = C * s + j
                if third == 0:
                    pe.wait_ge(s_yl, 2 * n + 2)
                    if is_end(t, b):
                        pe.wait_ge(s_sg, G * n + 1)
                    elif j == 0:
                        pe.wait_ge(s_pre, M * (s + 1) + 7)
                    else:
                        pe.wait_ge(s_res, n)
                y = (ygh, ygl)
                last = three(ps_r[:, 0, :], lambda a, k: y[a][:, k, :], lambda c, k: wo[c][:, k, :], M, 3 * third, min(3 * third + 3, M))
                if third == 2:
                    last.then_inc(s_op, 1)

            def rest(t, b, fill):
                s = B * t + b
                pe.wait_ge(s_dta, 3 * s + 3)
                pe.wait_ge(s_mb, 2 * s + 2)
                wait(pe, s_stm, 4 * s)
                for g in range(G):
                    last = pe.matmul(ps_m[:, g * T:(g + 1) * T], spread_h[:, g].rearrange("k h n -> k (h n)"), e,
                                     start=True, stop=True)
                last.then_inc(s_dr, 1)
                fill(0)
                pe.wait_ge(s_cs, s + 1)
                pe.wait_ge(s_ec, 4 * s + 4)
                pe.matmul(ps_m[:, 0:T], spread_n.rearrange("k h n -> k (h n)"), cs[:, b, :], start=True, stop=True).then_inc(s_cr, 1)
                fill(1)
                pe.wait_ge(s_dtr, s + 1)
                pe.wait_ge(s_cx, s + 1)
                for j in range(C):
                    last = pe.transpose(ps_m[:, j * P:(j + 1) * P], bcs[:, b, j * P:(j + 1) * P], ident)
                last.then_inc(s_btp, 1)
                fill(2)

            steps(pe, turn=turn, lead=lead, front=front, ssm=ssm, rest=rest, x_part=x_part, z_part=z_part, o_part=o_part)


def bounded_ffn(nc, signals, x_in, x_out, w, scale, fill, space_end, ahead):
    C = 4
    T = C * P
    NT = x_in.shape[0] // C
    TINY = 1e-7
    LIMIT = 0.99
    with ExitStack() as ctx:
        def ps(name, shape):
            return ctx.enter_context(nc.psum_tensor(name, shape, F32))[:]

        def sem(name):
            return signals(name)

        sb = Sbuf(nc, SBUF_START, space_end)
        ident = sb("b_ident", [P, P], F32)
        eps = sb("b_eps", [P, 1], F32)
        hold = sb("b_hold", [P, 1], F32)
        stats = sb("b_stats", [P, C, 6], F32)
        mv = sb("b_mv", [P, C, 2], F32)
        std = sb("b_std", [P, C], F32)
        ssq = sb("b_ssq", [P, C], F32)
        nrm = sb("b_nrm", [P, C], F32)
        nm = sb("b_nm", [P, C], F32)
        th = sb("b_th", [P, C], F32)
        f = sb("b_f", [P, C], F32)
        g = sb("b_g", [P, C], F32)
        scl = sb("b_scl", [P, D], F32)
        wh = sb("b_wh", [P, KD, D], F32R)
        wl = sb("b_wl", [P, KD, D], F32R)
        stage = sb("b_stage", [P, KD, D], F32)
        xth = sb("b_xth", [P, KD, T], F32R)
        xtl = sb("b_xtl", [P, KD, T], F32R)
        xin = sb("b_xin", [P, C, D], F32)
        o = sb("b_o", [P, C, D], F32)
        sq = sb("b_sq", [P, C, D], F32)

        ps_t = ps("b_pst", [P, 2, KD, P])
        ps_o = ps("b_pso", [P, C, D])

        s_small = sem("b_small")
        s_const = sem("b_const")
        s_stage = sem("b_stage_in")
        s_whi = sem("b_whi")
        s_wlo = sem("b_wlo")
        s_x = [sem(f"b_x{c}") for c in range(C)]
        s_xt = sem("b_xt")
        s_xh = sem("b_xh")
        s_xl = sem("b_xl")
        s_mm = sem("b_mm")
        s_o = sem("b_o_done")
        s_ssq = sem("b_ssq_done")
        s_nrm = sem("b_nrm_done")
        s_th = sem("b_th_done")
        s_res = sem("b_res")
        s_bn = sem("b_bn")
        s_var = sem("b_var")
        s_std = sem("b_std_done")
        s_ln = sem("b_ln")
        s_chain = sem("b_chain")
        s_st = [sem(f"b_st{c}") for c in range(C)]

        def chunk(dram, t, c):
            return dram[bass.ds(t * C + c, 1), :, :].rearrange("a p d -> p (a d)")

        block = ctx.enter_context(nc.Block())

        @block.sync
        def _(sp):
            sp.dma_start(scl, scale.partition_broadcast(P)).then_inc(s_small, 16)

            def load_x(t):
                for c in range(C):
                    wait(sp, s_res, C * (t - 1) + c + 1)
                    sp.dma_start(xin[:, c, :], chunk(x_in, t, c)).then_inc(s_x[c], 16)

            load_x(0)
            sp.dma_start(stage, w.rearrange("(k p) n -> p k n", p=P)).then_inc(s_stage, 16)
            for dst, src, arrived in ahead:
                sp.dma_start(dst, src).then_inc(arrived, 16)

            def store(t):
                for c in range(C):
                    sp.wait_ge(s_ln, C * t + c + 1)
                    sp.dma_start(chunk(x_out, t, c), o[:, c, :]).then_inc(s_st[c], 16)

            with sp.Fori(1, NT) as t:
                load_x(t)
                store(t - 1)
            store(NT - 1)
            for c in range(C):
                sp.wait_ge(s_st[c], 16 * NT)

        @block.gpsimd
        def _(pool):
            fill(pool, ident, s_const)
            pool.memset(eps, EPS).then_inc(s_const, 1)

        @block.scalar
        def _(act):
            act.wait_ge(s_const, 3)
            act.wait_ge(s_stage, 16)
            act.activation(wh, stage, ACT.Copy).then_inc(s_whi, 1)

            def step(t):
                for c in range(C):
                    act.wait_ge(s_xt, C * t + c + 1)
                    act.activation(xth[:, :, c * P:(c + 1) * P], ps_t[:, c % 2, :, :], ACT.Copy).then_inc(s_xh, 1)
                for c in range(C):
                    act.wait_ge(s_o, C * t + c + 1)
                    act.activation(sq[:, c, :], o[:, c, :], ACT.Square, accum_out=ssq[:, c:c + 1]).then_inc(s_ssq, 1)
                act.wait_ge(s_ssq, C * t + C)
                act.activation(nrm, ssq, ACT.Sqrt).then_inc(s_nrm, 1)
                act.wait_ge(s_nrm, 2 * t + 2)
                act.activation(th, nm, ACT.Tanh).then_inc(s_th, 1)
                act.wait_ge(s_var, C * t + C)
                act.activation(std, mv[:, :, 1], ACT.Sqrt, bias=eps).then_inc(s_std, 1)

            tiles(act, NT, step)

        @block.vector
        def _(dve):
            dve.wait_ge(s_whi, 1)
            dve.tensor_tensor(wl, stage, wh.bitcast(F32), ALU.subtract).then_inc(s_wlo, 1)
            dve.wait_ge(s_small, 16)

            def step(t):
                link = chain(dve, s_chain, 9 * t)
                for c in range(C):
                    dve.wait_ge(s_xh, C * t + c + 1)
                    cols = slice(c * P, (c + 1) * P)
                    dve.tensor_tensor(xtl[:, :, cols], ps_t[:, c % 2, :, :], xth[:, :, cols].bitcast(F32), ALU.subtract).then_inc(s_xl, 1)
                for c in range(C):
                    dve.wait_ge(s_mm, C * t + c + 1)
                    wait(dve, s_st[c], 16 * t)
                    dve.tensor_tensor(o[:, c, :], ps_o[:, c, :], scl, ALU.mult).then_inc(s_o, 1)
                dve.wait_ge(s_nrm, 2 * t + 1)
                dve.tensor_scalar(nm, nrm, TINY, None, ALU.max).then_inc(s_nrm, 1)
                dve.wait_ge(s_nrm, 2 * t + 2)
                link(dve.tensor_scalar(f, nm, TINY, None, ALU.add))
                link(dve.reciprocal(f, f))
                dve.wait_ge(s_th, t + 1)
                link(dve.tensor_tensor(f, f, th, ALU.mult))
                link(dve.tensor_tensor(g, f, nrm, ALU.mult))
                link(dve.tensor_scalar(g, g, TINY, None, ALU.max))
                link(dve.reciprocal(g, g))
                link(dve.tensor_scalar(g, g, LIMIT, 1.0, ALU.mult, ALU.min))
                link(dve.tensor_tensor(f, f, g, ALU.mult))
                for c in range(C):
                    dve.scalar_tensor_tensor(out=o[:, c, :], in0=o[:, c, :], scalar=f[:, c:c + 1], in1=xin[:, c, :],
                                             op0=ALU.mult, op1=ALU.add).then_inc(s_res, 1)
                for c in range(C):
                    dve.wait_ge(s_res, C * t + c + 1)
                    dve.bn_stats(stats[:, c, :], o[:, c, :]).then_inc(s_bn, 1)
                dve.wait_ge(s_bn, C * t + C)
                dve.memset(hold, 0.0)
                for c in range(C):
                    dve.bn_aggr(mv[:, c, :], stats[:, c, :]).then_inc(s_var, 1)
                dve.wait_ge(s_std, t + 1)
                link(dve.reciprocal(std, std))
                for c in range(C):
                    dve.tensor_scalar(o[:, c, :], o[:, c, :], mv[:, c, 0:1], std[:, c:c + 1], ALU.subtract, ALU.mult).then_inc(s_ln, 1)

            tiles(dve, NT, step)

        @block.tensor
        def _(pe):
            pe.wait_ge(s_const, 3)

            def step(t):
                for c in range(C):
                    pe.wait_ge(s_x[c], 16 * t + 16)
                    wait(pe, s_xl, C * t + c - 1)
                    for k in range(KD):
                        last = pe.transpose(ps_t[:, c % 2, k, :], xin[:, c, k * P:(k + 1) * P], ident)
                    last.then_inc(s_xt, 1)
                pe.wait_ge(s_wlo, 1)
                for c in range(C):
                    pe.wait_ge(s_xl, C * t + c + 1)
                    wait(pe, s_o, C * (t - 1) + c + 1)
                    i = 0
                    for k in range(KD):
                        for x, wp in ((xth, wh), (xth, wl), (xtl, wh)):
                            last = pe.matmul(ps_o[:, c, :], x[:, k, c * P:(c + 1) * P], wp[:, k, :], start=i == 0, stop=i == 3 * KD - 1)
                            i += 1
                    last.then_inc(s_mm, 1)

            tiles(pe, NT, step)


def rg_lru(nc, signals, x_in, x_out, vectors, b_out, fill, raw, s_raw, space_end, ahead):
    T = 256
    B = 2
    C = T // P
    NT = x_in.shape[0] // (B * C)
    M = KD
    with ExitStack() as ctx:
        def ps(name, shape):
            return ctx.enter_context(nc.psum_tensor(name, shape, F32))[:]

        def sem(name):
            return signals(name)

        sb = Sbuf(nc, SBUF_START, space_end)
        ident = sb("c_ident", [P, P], F32)
        vec = sb("c_vec", [P, 10, M], F32)
        BX, BY, BIG, BAG, CB, AP, W0 = range(7)
        spt = sb("c_spt", [P, 6, M], F32)
        eps = sb("c_eps", [P, 1], F32)
        hold = sb("c_hold", [P, 1], F32)
        stats = sb("c_stats", [P, C, 6], F32)
        mv = sb("c_mv", [P, C, 4], F32)
        bo = sb("c_bo", [P, D], F32)
        W = {}
        for n in ("x", "y", "ig", "ag", "out"):
            W[n] = (sb(f"c_w{n}h", [P, KD, D], F32R), sb(f"c_w{n}l", [P, KD, D], F32R))
        xth = sb("c_xth", [P, B, KD, T], F32R)
        xtl = sb("c_xtl", [P, B, KD, T], F32R)
        cvh = sb("c_cvh", [P, M, T], F32R)
        cvl = sb("c_cvl", [P, M, T], F32R)
        hyh = sb("c_hyh", [P, M, T], F32R)
        hyl = sb("c_hyl", [P, M, T], F32R)
        xin = sb("c_xin", [P, B * C, D], F32)
        xpre = sb("c_xpre", [P, M, T + 3], F32)
        carry = sb("c_carry", [P, B, M, 3], F32)
        zero3 = sb("c_zero3", [P, M, 3], F32)
        hlast = sb("c_hlast", [P, B, M, 1], F32)
        cv = sb("c_cv", [P, M, T], F32)
        y = sb("c_y", [P, B, M, T], F32)
        gx = sb("c_gx", [P, M, T], F32)
        a = sb("c_a", [P, M, T], F32)
        mu = sb("c_mu", [P, M, T], F32)
        hs = sb("c_hs", [P, M, T], F32)
        r = sb("c_r", [P, C, D], F32)

        ps_t = ps("c_pst", [P, C, KD, P])
        ps_a = ps("c_psa", [P, 2, 2, T])
        ps_b = ps("c_psb", [P, 2, 2, T])
        ps_o = ps("c_pso", [P, C, D])

        s_small = sem("c_small")
        s_const = sem("c_const")
        s_whi = sem("c_whi")
        s_wlo = sem("c_wlo")
        s_sp = sem("c_sp")
        s_sp_act = sem("c_sp_act")
        s_x = [sem(f"c_x{i}") for i in range(B * C)]
        s_xt = sem("c_xt")
        s_xh = sem("c_xh")
        s_xl = sem("c_xl")
        s_xb = sem("c_xb")
        s_pre = sem("c_pre")
        s_edge = sem("c_edge")
        s_keep = sem("c_keep")
        s_acc = sem("c_acc")
        s_conv = sem("c_conv")
        s_cvh = sem("c_cvh")
        s_cvl = sem("c_cvl")
        s_yp = sem("c_yp")
        s_y = sem("c_y")
        s_ig = sem("c_ig")
        s_ag = sem("c_ag")
        s_gx = sem("c_gx")
        s_ga = sem("c_ga")
        s_a = sem("c_a")
        s_a2 = sem("c_a2")
        s_gc = sem("c_gc")
        s_one = sem("c_one")
        s_mu = sem("c_mu")
        s_scan = sem("c_scan")
        s_hy = sem("c_hy")
        s_hyh = sem("c_hyh")
        s_hyl = sem("c_hyl")
        s_bo = sem("c_bo")
        s_out = sem("c_out")
        s_res = sem("c_res")
        s_var = sem("c_var")
        s_std = sem("c_std")
        s_ln = sem("c_ln")
        s_chain = sem("c_chain")
        s_hchain = sem("c_hchain")
        s_cchain = sem("c_cchain")
        s_st = [sem(f"c_st{i}") for i in range(C)]

        pieces = []
        for i, n in enumerate(W):
            for k in (0, 2):
                pieces.append((raw[:, i, k:k + 2, :], s_raw[i], W[n][0][:, k:k + 2, :], W[n][1][:, k:k + 2, :]))

        def chunk(dram, t, b, j):
            return dram[bass.ds(t * C + (b * NT * C + j), 1), :, :].rearrange("a p d -> p (a d)")

        def steps(eng, step, after=None):
            for b in range(B):
                step(0, b)
            with eng.Fori(1, NT) as t:
                for b in range(B):
                    step(t, b)
            if after:
                after()

        block = ctx.enter_context(nc.Block())

        @block.sync
        def _(sp):
            sp.dma_start(vec, vectors).then_inc(s_small, 16)
            sp.dma_start(bo, b_out.partition_broadcast(P)).then_inc(s_small, 16)

            def load_x(t, b):
                for j in range(C):
                    wait(sp, s_res, C * (2 * t + b) - 2 * C + j + 1)
                    sp.dma_start(xin[:, b * C + j, :], chunk(x_in, t, b, j)).then_inc(s_x[b * C + j], 16)

            def store(t, b):
                s = 2 * t + b
                for j in range(C):
                    sp.wait_ge(s_ln, C * s + j + 1)
                    sp.dma_start(chunk(x_out, t, b, j), r[:, j, :]).then_inc(s_st[j], 16)

            load_x(0, 0)
            load_x(0, 1)
            sp.wait_ge(s_wlo, len(pieces))
            for dst, src, arrived in ahead:
                sp.dma_start(dst, src).then_inc(arrived, 16)

            with sp.Fori(1, NT) as t:
                for b in range(B):
                    load_x(t, b)
                    store(t - 1, b)
            for b in range(B):
                store(NT - 1, b)
            for j in range(C):
                sp.wait_ge(s_st[j], 16 * NT * B)

        @block.gpsimd
        def _(pool):
            fill(pool, ident, s_const)
            pool.memset(eps, EPS).then_inc(s_const, 1)
            pool.memset(zero3, 0.0).then_inc(s_const, 1)
            pool.memset(hlast, 0.0).then_inc(s_const, 1)
            pool.wait_ge(s_const, 5)
            pool.wait_ge(s_small, 32)

            def step(t, b):
                s = 2 * t + b
                wait(pool, s_conv, s)
                wait(pool, s_keep, s)
                if isinstance(t, int):
                    pool.memset(xpre[:, :, 0:3], 0.0).then_inc(s_edge, 1)
                else:
                    pool.tensor_tensor(xpre[:, :, 0:3], carry[:, b], zero3, ALU.add).then_inc(s_edge, 1)
                pool.wait_ge(s_edge, s + 1)
                pool.wait_ge(s_pre, M * s + M)
                pool.tensor_tensor(carry[:, b], xpre[:, :, T:T + 3], zero3, ALU.add).then_inc(s_keep, 1)
                pool.wait_ge(s_cvh, s + 1)
                pool.tensor_tensor(cvl, cv, cvh.bitcast(F32), ALU.subtract).then_inc(s_cvl, 1)
                for j in range(C):
                    pool.wait_ge(s_x[b * C + j], 16 * t + 16)
                    pool.wait_ge(s_xt, C * s + j + 1)
                    pool.tensor_tensor(xin[:, b * C + j, :], xin[:, b * C + j, :], bo, ALU.add).then_inc(s_bo, 1)
                pool.wait_ge(s_gx, M * s + M)
                pool.tensor_tensor(gx, gx, cv, ALU.mult).then_inc(s_gc, 1)
                pool.wait_ge(s_a, M * s + M)
                if isinstance(t, int):
                    wait(pool, s_hchain, s)
                    pool.memset(mu[:, :, 0:1], 1.0).then_inc(s_one, 1)
                    pool.wait_ge(s_one, s + 1)
                    pool.tensor_tensor(mu[:, :, 1:T], a[:, :, 1:T], a[:, :, 1:T], ALU.mult).then_inc(s_a2, 1)
                else:
                    pool.tensor_tensor(mu, a, a, ALU.mult).then_inc(s_a2, 1)

            steps(pool, step)

        @block.scalar
        def _(act):
            act.wait_ge(s_small, 32)
            act.wait_ge(s_const, 5)
            for piece, arrived, hi, _ in pieces:
                act.wait_ge(arrived, 16)
                act.activation(hi, piece, ACT.Copy).then_inc(s_whi, 1)
            act.wait_ge(s_sp, 1)
            act.activation(spt[:, 0, :], spt[:, 0, :], ACT.Exp).then_inc(s_sp_act, 1)
            act.wait_ge(s_sp, 2)
            act.activation(spt[:, 2, :], spt[:, 1, :], ACT.Ln).then_inc(s_sp_act, 1)
            act.wait_ge(s_sp, 10)
            act.wait_ge(s_wlo, len(pieces))

            def high_hy(t, b):
                act.wait_ge(s_hy, 2 * t + b + 1)
                act.activation(hyh, hs, ACT.Copy).then_inc(s_hyh, 1)

            def std(t, b):
                s = 2 * t + b
                for j in range(C):
                    act.wait_ge(s_var, C * s + j + 1)
                    act.activation(mv[:, j, 2:3], mv[:, j, 1:2], ACT.Sqrt, bias=eps).then_inc(s_std, 1)

            def step(t, b):
                s = 2 * t + b
                prev = (t, 0) if b else (t - 1, 1)
                first = isinstance(t, int) and s == 0
                for j in range(C):
                    act.wait_ge(s_xt, C * s + j + 1)
                    act.activation(xth[:, b, :, j * P:(j + 1) * P], ps_t[:, j, :, :], ACT.Copy).then_inc(s_xh, 1)
                wait(act, s_conv, s)
                wait(act, s_keep, s)
                for m in range(M):
                    act.wait_ge(s_xb, 2 * s + m // 2 + 1)
                    act.activation(xpre[:, m, 3:T + 3], ps_a[:, m // 2, m % 2, :], ACT.Identity,
                                   bias=vec[:, BX, m:m + 1]).then_inc(s_pre, 1)
                wait(act, s_gc, s)
                act.wait_ge(s_pre, M * s + M)
                for m in range(M):
                    act.activation(cv[:, m, :], xpre[:, m, 3:T + 3], ACT.Identity, bias=vec[:, CB, m:m + 1],
                                   scale=vec[:, W0 + 3, m:m + 1]).then_inc(s_acc, 1)
                if not first:
                    high_hy(*prev)
                for m in range(M):
                    act.wait_ge(s_yp, 2 * s + m // 2 + 1)
                    wait(act, s_hy, s - 1)
                    act.activation(y[:, b, m, :], ps_a[:, m // 2, m % 2, :], ACT.Gelu, bias=vec[:, BY, m:m + 1]).then_inc(s_y, 1)
                act.wait_ge(s_conv, s + 1)
                act.activation(cvh, cv, ACT.Copy).then_inc(s_cvh, 1)
                if not first:
                    std(*prev)
                for m in range(M):
                    act.wait_ge(s_ig, 2 * s + m // 2 + 1)
                    wait(act, s_hy, s)
                    act.activation(gx[:, m, :], ps_b[:, m // 2, m % 2, :], ACT.Sigmoid, bias=vec[:, BIG, m:m + 1]).then_inc(s_gx, 1)
                for m in range(M):
                    act.wait_ge(s_ag, 2 * s + m // 2 + 1)
                    act.activation(a[:, m, :], ps_b[:, m // 2, m % 2, :], ACT.Sigmoid, bias=vec[:, BAG, m:m + 1]).then_inc(s_ga, 1)
                act.wait_ge(s_ga, M * s + M)
                for m in range(M):
                    act.activation(a[:, m, :], a[:, m, :], ACT.Exp, scale=spt[:, 5, m:m + 1]).then_inc(s_a, 1)
                act.wait_ge(s_a2, s + 1)
                left = mu[:, :, 1:T] if isinstance(t, int) else mu
                act.activation(left, left, ACT.Sqrt, scale=-1.0, bias=1.0).then_inc(s_mu, 1)

            def last():
                high_hy(NT - 1, 1)
                std(NT - 1, 1)

            steps(act, step, last)

        @block.vector
        def _(dve):
            dve.wait_ge(s_small, 32)
            dve.wait_ge(s_const, 5)
            for i, (piece, _, hi, lo) in enumerate(pieces):
                dve.wait_ge(s_whi, i + 1)
                dve.tensor_tensor(lo, piece, hi.bitcast(F32), ALU.subtract).then_inc(s_wlo, 1)
            z = vec[:, AP, :]
            e, u, l, one, q, scale = (spt[:, i, :] for i in range(6))
            link = chain(dve, s_sp, 0)
            link(dve.scalar_tensor_tensor(out=e, in0=z, scalar=-1.0, in1=z, op0=ALU.mult, op1=ALU.min))
            dve.wait_ge(s_sp_act, 1)
            link(dve.tensor_scalar(u, e, 1.0, None, ALU.add))
            dve.wait_ge(s_sp_act, 2)
            link(dve.tensor_scalar(one, u, 1.0, None, ALU.is_equal))
            link(dve.scalar_tensor_tensor(out=q, in0=u, scalar=-1.0, in1=one, op0=ALU.add, op1=ALU.add))
            link(dve.reciprocal(q, q))
            link(dve.tensor_tensor(q, q, l, ALU.mult))
            link(dve.tensor_tensor(q, q, one, ALU.add))
            link(dve.tensor_tensor(q, q, e, ALU.mult))
            link(dve.scalar_tensor_tensor(out=q, in0=z, scalar=0.0, in1=q, op0=ALU.max, op1=ALU.add))
            link(dve.tensor_scalar(scale, q, -8.0, None, ALU.mult))

            def recur(t, b):
                s = 2 * t + b
                dve.wait_ge(s_mu, s + 1)
                dve.wait_ge(s_gc, s + 1)
                dve.tensor_tensor(gx, gx, mu, ALU.mult).then_inc(s_hchain, 1)
                dve.wait_ge(s_hchain, s + 1)
                wait(dve, s_hyh, s)
                for m in range(M):
                    dve.tensor_tensor_scan(hs[:, m, :], a[:, m, :], gx[:, m, :],
                                           hlast[:, b, m, :],
                                           ALU.mult, ALU.add).then_inc(s_scan, 1)
                dve.wait_ge(s_scan, (M + 1) * s + M)
                dve.tensor_copy(hlast[:, b], hs[:, :, T - 1:T]).then_inc(s_scan, 1)
                dve.wait_ge(s_scan, (M + 1) * s + M + 1)
                dve.wait_ge(s_y, M * s + M)
                dve.tensor_tensor(hs, hs, y[:, b], ALU.mult).then_inc(s_hy, 1)
                dve.wait_ge(s_hyh, s + 1)
                dve.tensor_tensor(hyl, hs, hyh.bitcast(F32), ALU.subtract).then_inc(s_hyl, 1)

            def norm(t, b):
                s = 2 * t + b
                link = chain(dve, s_chain, 2 * C * s)
                for j in range(C):
                    out = r[:, j, :]
                    dve.wait_ge(s_out, C * s + j + 1)
                    dve.wait_ge(s_bo, C * s + j + 1)
                    wait(dve, s_st[j], 16 * s)
                    dve.tensor_tensor(out, ps_o[:, j, :], xin[:, b * C + j, :], ALU.add).then_inc(s_res, 1)
                    dve.wait_ge(s_res, C * s + j + 1)
                    link(dve.bn_stats(stats[:, j, :], out))
                    dve.memset(hold, 0.0)
                    dve.bn_aggr(mv[:, j, 0:2], stats[:, j, :]).then_inc(s_var, 1)
                for j in range(C):
                    out = r[:, j, :]
                    dve.wait_ge(s_std, C * s + j + 1)
                    link(dve.reciprocal(mv[:, j, 3:4], mv[:, j, 2:3]))
                    dve.tensor_scalar(out, out, mv[:, j, 0:1], mv[:, j, 3:4], ALU.subtract, ALU.mult).then_inc(s_ln, 1)

            def step(t, b):
                s = 2 * t + b
                prev = (t, 0) if b else (t - 1, 1)
                first = isinstance(t, int) and s == 0
                for j in range(C):
                    dve.wait_ge(s_xh, C * s + j + 1)
                    cols = slice(j * P, (j + 1) * P)
                    dve.tensor_tensor(xtl[:, b, :, cols], ps_t[:, j, :, :], xth[:, b, :, cols].bitcast(F32), ALU.subtract).then_inc(s_xl, 1)
                if not first:
                    recur(*prev)
                dve.wait_ge(s_edge, s + 1)
                dve.wait_ge(s_acc, M * s + M)
                for k in range(3):
                    for m in range(M):
                        ins = dve.scalar_tensor_tensor(out=cv[:, m, :], in0=xpre[:, m, k:k + T], scalar=vec[:, W0 + k, m:m + 1],
                                                       in1=cv[:, m, :], op0=ALU.mult, op1=ALU.add)
                        if k < 2:
                            ins.then_inc(s_cchain, 1)
                        elif m == M - 1:
                            ins.then_inc(s_conv, 1)
                    if k < 2:
                        dve.wait_ge(s_cchain, 2 * M * s + M * (k + 1))
                if not first:
                    norm(*prev)

            def last():
                recur(NT - 1, 1)
                norm(NT - 1, 1)

            steps(dve, step, last)

        @block.tensor
        def _(pe):
            pe.wait_ge(s_const, 5)

            def project(ps_x, w, xh, xl, s, free, done):
                for q in range(2):
                    free(q)
                    for m in (2 * q, 2 * q + 1):
                        i = 0
                        for k in range(KD):
                            for wp, x in ((w[0], xh), (w[0], xl), (w[1], xh)):
                                last = pe.matmul(ps_x[:, q, m % 2, :], wp[:, k, m * P:(m + 1) * P], x[:, k, :],
                                                 start=i == 0, stop=i == 3 * KD - 1)
                                i += 1
                    last.then_inc(done, 1)

            def output(t, b):
                s = 2 * t + b
                pe.wait_ge(s_hyl, s + 1)
                for j in range(C):
                    wait(pe, s_res, C * (s - 1) + j + 1)
                    i = 0
                    for k in range(KD):
                        for h, wp in ((hyh, W["out"][0]), (hyh, W["out"][1]), (hyl, W["out"][0])):
                            last = pe.matmul(ps_o[:, j, :], h[:, k, j * P:(j + 1) * P], wp[:, k, :], start=i == 0, stop=i == 3 * KD - 1)
                            i += 1
                    last.then_inc(s_out, 1)

            def step(t, b):
                s = 2 * t + b
                first = isinstance(t, int) and s == 0
                for j in range(C):
                    pe.wait_ge(s_x[b * C + j], 16 * t + 16)
                    wait(pe, s_xl, C * (s - 1) + j + 1)
                    for k in range(KD):
                        last = pe.transpose(ps_t[:, j, k, :], xin[:, b * C + j, k * P:(k + 1) * P], ident)
                    last.then_inc(s_xt, 1)
                pe.wait_ge(s_xl, C * s + C)
                if first:
                    pe.wait_ge(s_wlo, len(pieces))
                project(ps_a, W["x"], xth[:, b], xtl[:, b], s, lambda q: wait(pe, s_y, M * (s - 1) + 2 * q + 2), s_xb)
                project(ps_a, W["y"], xth[:, b], xtl[:, b], s, lambda q: wait(pe, s_pre, M * s + 2 * q + 2), s_yp)
                if not first:
                    output(*((t, 0) if b else (t - 1, 1)))
                pe.wait_ge(s_cvl, s + 1)
                project(ps_b, W["ig"], cvh, cvl, s, lambda q: wait(pe, s_ga, M * (s - 1) + 2 * q + 2), s_ig)
                project(ps_b, W["ag"], cvh, cvl, s, lambda q: wait(pe, s_gx, M * s + 2 * q + 2), s_ag)

            steps(pe, step, lambda: output(NT - 1, 1))


ZERO_POINT = 128.0


def ffn_codes(nc, gate_wt, up_wt):
    ff = gate_wt.shape[1]
    start = SBUF_END - 4 * KD * (ff + ff // 2)
    sb = Sbuf(nc, start, SBUF_END)
    up = sb("d_wu_early_codes", [P, KD, ff // 2], I32)
    gate = sb("d_wg_codes", [P, KD, ff], I32)
    transfers = []
    for k in range(KD):
        transfers.append((gate[:, k, :], gate_wt[k * P:(k + 1) * P, :]))
        transfers.append((up[:, k, :], up_wt[k * P:(k + 1) * P, 0:ff // 2]))
    return (start, up, gate, 16 * len(transfers)), transfers


def gated_ffn(nc, signals, x_in, x_out, gate_wt, up_wt, down_wt, gate_scale, up_scale, down_scale, ident_fill, codes, s_codes):
    T = 512
    NT = x_in.shape[0] * P // T
    C = T // P
    FF = gate_wt.shape[1]
    M = FF // P
    with ExitStack() as ctx:
        def ps(name, shape):
            return ctx.enter_context(nc.psum_tensor(name, shape, F32))[:]

        def sem(name):
            return signals(name)

        sb = Sbuf(nc, SBUF_START, codes[0])
        ident = sb("d_ident", [P, P], F32)
        gs = sb("d_gs", [P, M], F32)
        us = sb("d_us", [P, M], F32)
        half = sb("d_half", [P, 2], F32)
        hold = sb("d_hold", [P, 1], F32)
        stats = sb("d_stats", [P, 2, 6], F32)
        mv = sb("d_mv", [P, 2, 4], F32)
        dsb = sb("d_dsb", [P, D], F32)
        half_ff = FF // 2
        late = sb.at
        wu_late = sb("d_wu_late", [P, KD, half_ff], F32R)
        wd = sb("d_wd", [P, M, D], F32R)
        sb_late = Sbuf(nc, late, sb.at)
        wu_late_codes = sb_late("d_wu_late_codes", [P, KD, half_ff], I32)
        wd_codes = sb_late("d_wd_codes", [P, M, D], I32)
        sb_early = Sbuf(nc, codes[0], SBUF_END)
        wu_early = sb_early("d_wu_early", [P, KD, half_ff], F32R)
        wg = sb_early("d_wg", [P, KD, FF], F32R)
        xth = sb("d_xth", [P, KD, T], F32R)
        xtl = sb("d_xtl", [P, KD, T], F32R)
        hh = sb("d_hh", [P, M, T], F32R)
        hl = sb("d_hl", [P, M, T], F32R)
        xin = sb("d_xin", [P, C, D], F32)
        sg = sb("d_sg", [P, 2, T], F32)
        h32 = sb("d_h32", [P, 2, T], F32)
        tmp = sb("d_tmp", [P, 2, D], F32)
        r = sb("d_r", [P, 2, D], F32)

        ps_t = ps("d_pst", [P, 2, KD, P])
        ps_g = ps("d_psg", [P, 2, T])
        ps_u = ps("d_psu", [P, 2, T])
        ps_o = ps("d_pso", [P, 2, D])

        s_small = sem("d_small")
        s_const = sem("d_const")
        s_prep, s_prep_down = sem("d_prep"), sem("d_prep_down")
        s_up_late, s_down = sem("d_up_late"), sem("d_down")
        s_x = [sem(f"d_x{c}") for c in range(C)]
        s_xt = sem("d_xt")
        s_xh = sem("d_xh")
        s_xl = sem("d_xl")
        s_g = sem("d_g")
        s_u = sem("d_u")
        s_sg = sem("d_sg")
        s_h = sem("d_h")
        s_hh = sem("d_hh")
        s_hl = sem("d_hl")
        s_dn = sem("d_dn")
        s_res = sem("d_res")
        s_var = sem("d_var")
        s_eps = sem("d_eps")
        s_std = sem("d_std")
        s_ln = sem("d_ln")
        s_chain = sem("d_chain")
        s_st = [sem(f"d_st{i}") for i in range(2)]
        s_r = [sem(f"d_r{i}") for i in range(2)]

        pieces = []
        for m in range(0, M, 2):
            cols = slice(m * P, (m + 2) * P)
            pieces.append((wg[:, :, cols], codes[2][:, :, cols], s_codes, codes[3]))
            if m < M // 2:
                pieces.append((wu_early[:, :, cols], codes[1][:, :, cols], s_codes, codes[3]))
            else:
                own = slice(m * P - half_ff, (m + 2) * P - half_ff)
                pieces.append((wu_late[:, :, own], wu_late_codes[:, :, own], s_up_late, 16 * KD))
        for m in range(0, M, 2):
            pieces.append((wd[:, m:m + 2, :], wd_codes[:, m:m + 2, :], s_down, 16 * KD))

        def gate_cols(k, m):
            return wg[:, k, m * P:(m + 1) * P]

        def up_cols(k, m):
            return wu_early[:, k, m * P:(m + 1) * P] if m < M // 2 else wu_late[:, k, m * P - half_ff:(m + 1) * P - half_ff]

        def pipelined(eng, front, step):
            front(0)
            step(0, True)
            with eng.Fori(1, NT - 1) as t:
                step(t, True)
            step(NT - 1, False)

        block = ctx.enter_context(nc.Block())

        @block.sync
        def _(sp):
            sp.dma_start(gs, gate_scale).then_inc(s_small, 16)
            sp.dma_start(us, up_scale).then_inc(s_small, 16)
            sp.dma_start(dsb, down_scale.partition_broadcast(P)).then_inc(s_small, 16)

            def chunk(dram, t, c):
                return dram[bass.ds(t * C + c, 1), :, :].rearrange("a p d -> p (a d)")

            def load_x(t):
                for c in range(C):
                    wait(sp, s_xt, C * t - C + c + 1)
                    sp.dma_start(xin[:, c, :], chunk(x_in, t, c)).then_inc(s_x[c], 16)

            def load_r(t, c):
                wait(sp, s_st[c % 2], 16 * (2 * t + c // 2))
                sp.dma_start(r[:, c % 2, :], chunk(x_in, t, c)).then_inc(s_r[c % 2], 16)

            load_x(0)
            for k in range(KD):
                sp.dma_start(wu_late_codes[:, k, :], up_wt[k * P:(k + 1) * P, half_ff:FF]).then_inc(s_up_late, 16)
            for k in range(KD):
                rows = slice(k * M // KD, (k + 1) * M // KD)
                sp.dma_start(wd_codes[:, rows, :], down_wt.rearrange("(m p) n -> p m n", p=P)[:, rows, :]).then_inc(s_down, 16)

            def step(t, more):
                if more:
                    load_x(t + 1)
                load_r(t, 0)
                load_r(t, 1)
                for c in range(C):
                    sp.wait_ge(s_ln, C * t + c + 1)
                    sp.dma_start(chunk(x_out, t, c), r[:, c % 2, :]).then_inc(s_st[c % 2], 16)
                    if c + 2 < C:
                        load_r(t, c + 2)

            pipelined(sp, lambda t: None, step)
            for i in range(2):
                sp.wait_ge(s_st[i], 16 * NT * C // 2)

        @block.gpsimd
        def _(pool):
            ident_fill(pool, ident, s_const)
            pool.memset(half[:, 0:1], EPS)
            pool.memset(half[:, 1:2], -0.5).then_inc(s_const, 1)

            def step(t, more):
                for m in range(M):
                    pool.wait_ge(s_hh, M * t + m + 1)
                    pool.tensor_tensor(hl[:, m, :], h32[:, m % 2, :], hh[:, m, :].bitcast(F32), ALU.subtract).then_inc(s_hl, 1)
                for c in range(C):
                    v = mv[:, c % 2, 1:2]
                    pool.wait_ge(s_var, C * t + c + 1)
                    pool.tensor_tensor(v, v, half[:, 0:1], ALU.add).then_inc(s_eps, 1)
                    pool.wait_ge(s_eps, C * t + c + 1)
                    pool.tensor_tensor(mv[:, c % 2, 2:3], v, half[:, 1:2], ALU.pow).then_inc(s_std, 1)

            pipelined(pool, lambda t: None, step)

        @block.scalar
        def _(act):
            act.wait_ge(s_small, 48)
            act.wait_ge(s_const, 3)

            def high(t, m):
                act.wait_ge(s_h, M * t + m + 1)
                act.activation(hh[:, m, :], h32[:, m % 2, :], ACT.Copy).then_inc(s_hh, 1)

            def front(t):
                for c in range(C):
                    act.wait_ge(s_xt, C * t + c + 1)
                    act.activation(xth[:, :, c * P:(c + 1) * P], ps_t[:, c % 2, :, :], ACT.Copy).then_inc(s_xh, 1)

            def step(t, more):
                for m in range(M):
                    act.wait_ge(s_g, M * t + m + 1)
                    wait(act, s_h, M * t + m - 1)
                    act.activation(sg[:, m % 2, :], ps_g[:, m % 2, :], ACT.Silu, scale=gs[:, m:m + 1]).then_inc(s_sg, 1)
                    if m:
                        high(t, m - 1)
                high(t, M - 1)
                if more:
                    front(t + 1)

            pipelined(act, front, step)

        @block.vector
        def _(dve):
            def turn(i):
                dst, src, arrived, count = pieces[i]
                dve.wait_ge(arrived, count)
                dve.tensor_scalar(dst, src, -ZERO_POINT, None, ALU.add).then_inc(s_prep if i < M else s_prep_down, 1)

            turn(0)
            turn(1)
            dve.wait_ge(s_small, 48)

            def front(t):
                for c in range(C):
                    dve.wait_ge(s_xh, C * t + c + 1)
                    cols = slice(c * P, (c + 1) * P)
                    dve.tensor_tensor(xtl[:, :, cols], ps_t[:, c % 2, :, :], xth[:, :, cols].bitcast(F32), ALU.subtract).then_inc(s_xl, 1)

            def step(t, more):
                for m in range(M):
                    if isinstance(t, int) and t == 0:
                        if m % 2 == 0 and m + 2 < M:
                            turn(m + 2)
                            turn(m + 3)
                        if m >= M // 2:
                            turn(M + m - M // 2)
                    dve.wait_ge(s_sg, M * t + m + 1)
                    dve.wait_ge(s_u, M * t + m + 1)
                    wait(dve, s_hl, M * t + m - 1)
                    dve.scalar_tensor_tensor(out=h32[:, m % 2, :], in0=ps_u[:, m % 2, :], scalar=us[:, m:m + 1],
                                             in1=sg[:, m % 2, :], op0=ALU.mult, op1=ALU.mult).then_inc(s_h, 1)
                if more:
                    front(t + 1)
                link = chain(dve, s_chain, 2 * C * t)
                for c in range(C):
                    y = r[:, c % 2, :]
                    dve.wait_ge(s_dn, C * t + c + 1)
                    link(dve.tensor_tensor(tmp[:, c % 2, :], ps_o[:, c % 2, :], dsb, ALU.mult))
                    dve.wait_ge(s_r[c % 2], 16 * (2 * t + c // 2 + 1))
                    dve.tensor_tensor(y, y, tmp[:, c % 2, :], ALU.add).then_inc(s_res, 1)
                    dve.wait_ge(s_res, C * t + c + 1)
                    link(dve.bn_stats(stats[:, c % 2, :], y))
                    dve.memset(hold, 0.0)
                    dve.bn_aggr(mv[:, c % 2, 0:2], stats[:, c % 2, :]).then_inc(s_var, 1)
                    dve.wait_ge(s_std, C * t + c + 1)
                    dve.tensor_scalar(y, y, mv[:, c % 2, 0:1], mv[:, c % 2, 2:3], ALU.subtract, ALU.mult).then_inc(s_ln, 1)

            pipelined(dve, front, step)

        @block.tensor
        def _(pe):
            pe.wait_ge(s_const, 3)

            def front(t):
                for c in range(C):
                    pe.wait_ge(s_x[c], 16 * t + 16)
                    wait(pe, s_xl, C * t + c - 1)
                    for k in range(KD):
                        last = pe.transpose(ps_t[:, c % 2, k, :], xin[:, c, k * P:(k + 1) * P], ident)
                    last.then_inc(s_xt, 1)

            def step(t, more):
                pe.wait_ge(s_xl, C * t + C)
                for m in range(M):
                    if isinstance(t, int) and t == 0 and m % 2 == 0:
                        pe.wait_ge(s_prep, m + 2)
                    for out, w, done, used in ((ps_g, gate_cols, s_g, s_sg), (ps_u, up_cols, s_u, s_h)):
                        wait(pe, used, M * t + m - 1)
                        for k in range(KD):
                            for x in (xth, xtl):
                                last = pe.matmul(out[:, m % 2, :], w(k, m), x[:, k, :],
                                                 start=(k == 0 and x is xth), stop=(k == KD - 1 and x is xtl))
                        last.then_inc(done, 1)
                if more:
                    front(t + 1)
                if isinstance(t, int) and t == 0:
                    pe.wait_ge(s_prep_down, len(pieces) - M)
                pe.wait_ge(s_hl, M * t + M)
                for c in range(C):
                    wait(pe, s_res, C * t + c - 1)
                    for m in range(M):
                        for h in (hh, hl):
                            last = pe.matmul(ps_o[:, c % 2, :], h[:, m, c * P:(c + 1) * P], wd[:, m, :],
                                             start=(m == 0 and h is hh), stop=(m == M - 1 and h is hl))
                    last.then_inc(s_dn, 1)

            pipelined(pe, front, step)


def fill_identity(pool, ident, done):
    pool.memset(ident, 0.0).then_inc(done, 1)
    pool.wait_ge(done, 1)
    pool.affine_select(out=ident, in_=ident, compare_op=ALU.not_equal, fill=1.0, base=0,
                       pattern=[[-1, P]], channel_multiplier=1).then_inc(done, 1)




def build(nc, x, out, d):
    between = [nc.dram_tensor(f"tokens{i}", x.shape, F32, kind="Internal").ap() for i in range(3)]
    signals = Signals(nc)
    mamba2(nc, signals, x, between[0], d["w_x"], d["w_bc"], d["w_gate"], d["w_out0"], d["conv0"], d["A_log"], d["dt_bias"],
           d["D_skip"], d["norm_w"], fill_identity)
    signals.reset()
    raw = Sbuf(nc, SBUF_END - 4 * 5 * KD * D, SBUF_END)("c_raw", [P, 5, KD, D], F32)
    s_raw = [signals(f"c_raw{i}") for i in range(5)]
    weights = [(raw[:, i], d[name].rearrange("(k p) n -> p k n", p=P), s_raw[i])
               for i, name in enumerate(("w_in1", "w_y", "w_ig", "w_ag", "w_out1"))]
    codes, transfers = ffn_codes(nc, d["gate_w"], d["up_w"])
    s_codes = signals("d_codes")
    bounded_ffn(nc, signals, between[0], between[1], d["weight"], d["scale"], fill_identity, SBUF_END - 4 * 5 * KD * D, weights)
    rg_lru(nc, signals, between[1], between[2], d["vectors"], d["b_out"], fill_identity, raw, s_raw, codes[0],
           [(dst, src, s_codes) for dst, src in transfers])
    gated_ffn(nc, signals, between[2], out, d["gate_w"], d["up_w"], d["down_w"], d["gate_scale"], d["up_scale"], d["down_scale"],
              fill_identity, codes, s_codes)


def kernel(**inputs):
    import numpy as np
    import concourse.bacc as bacc
    from concourse.bass_utils import run_bass_kernel_spmd as run

    v = {name: np.asarray(a) for name, a in inputs.items()}
    nc = bacc.Bacc("TRN2", target_bir_lowering=False, num_devices=1)
    arrays, d = {}, {}

    def dram(name, a):
        a = np.ascontiguousarray(a)
        arrays["in_" + name] = a
        d[name] = nc.dram_tensor("in_" + name, a.shape, mybir.dt.from_np(a.dtype), kind="ExternalInput").ap()

    x = v["L0_attn_hidden_states"]
    dram("x", x.reshape(-1, P, D))

    w_in, conv_w, conv_b = v["L0_attn_W_in"], v["L0_attn_conv_w"], v["L0_attn_conv_b"]
    di, n, h = v["L0_attn_norm_w"].shape[0], 16, v["L0_attn_A_log"].shape[0]
    gap = np.zeros((D, 32 - n), w_in.dtype)
    dram("w_gate", w_in[:, :di])
    dram("w_x", w_in[:, di:2 * di])
    dram("w_bc", np.concatenate([w_in[:, 2 * di:2 * di + n], gap, w_in[:, 2 * di + n:2 * di + 2 * n], gap,
                                 w_in[:, 2 * di + 2 * n:], np.zeros((D, P - 64 - h), w_in.dtype)], axis=1))
    taps = np.concatenate([conv_w, conv_b[:, None]], axis=1)
    none = np.zeros((32 - n, taps.shape[1]), taps.dtype)
    rows = np.concatenate([taps[:di + n], none, taps[di + n:], none, np.zeros((64, taps.shape[1]), taps.dtype)])
    dram("conv0", rows.reshape(-1, P, taps.shape[1]).transpose(1, 0, 2))
    for name in ("A_log", "dt_bias", "D_skip"):
        dram(name, v["L0_attn_" + name])
    dram("norm_w", v["L0_attn_norm_w"].reshape(-1, P).T)
    dram("w_out0", v["L0_attn_W_out"])

    dram("weight", v["L0_ffn_weight"])
    dram("scale", v["L0_ffn_scale"])

    for name, key in (("w_in1", "w_x"), ("w_y", "w_y"), ("w_ig", "w_ig"), ("w_ag", "w_ag"), ("w_out1", "w_out"), ("b_out", "b_out")):
        dram(name, v["L1_attn_" + key])
    vectors = np.concatenate([np.stack([v["L1_attn_" + k] for k in ("b_x", "b_y", "b_ig", "b_ag", "conv_b", "a_param")]),
                              v["L1_attn_conv_w"]])
    dram("vectors", vectors.reshape(vectors.shape[0], KD, P).transpose(2, 0, 1))

    for name in ("gate_w", "up_w", "down_w"):
        dram(name, v["L1_ffn_" + name].T)
    for name in ("gate_scale", "up_scale"):
        dram(name, v["L1_ffn_" + name].reshape(-1, P).T)
    dram("down_scale", v["L1_ffn_down_scale"])

    out = nc.dram_tensor("out", arrays["in_x"].shape, F32, kind="ExternalOutput").ap()
    build(nc, d["x"], out, d)
    r = run(nc, [arrays], core_ids=[0])
    return r.results[0]["out"].reshape(x.shape)
```

```python
from contextlib import ExitStack

import concourse.bass as bass
from concourse import mybir

P = 128
D = 512
KD = D // P
F32 = mybir.dt.float32
F32R = mybir.dt.float32r
I32 = mybir.dt.int32
ACT = mybir.ActivationFunctionType
ALU = mybir.AluOpType
EPS = 1e-5
SBUF_START = 16512
SBUF_END = 229344


class Sbuf:

    def __init__(self, nc, start, end):
        self.nc, self.at, self.end = nc, start, end

    def __call__(self, name, shape, dtype):
        size = 2 if dtype == mybir.dt.bfloat16 else 4
        for n in shape[1:]:
            size *= n
        size = (size + 7) // 8 * 8
        assert self.at + size <= self.end, (name, self.at + size - self.end)
        t = self.nc.alloc_sbuf_tensor_at(name, shape, dtype, offset=self.at, align_bytes=8)
        self.at += size
        return t[:]


class Signals:

    def __init__(self, nc):
        self.nc, self.taken = nc, []

    def __call__(self, name):
        self.taken.append(self.nc.alloc_semaphore(name=name))
        return self.taken[-1]

    def reset(self):
        self.nc.clear_and_free_semaphores(self.taken)
        self.nc.all_engine_barrier()
        self.taken = []


def chain(eng, sem, base):
    count = [0]

    def link(ins):
        count[0] += 1
        ins.then_inc(sem, 1)
        eng.wait_ge(sem, base + count[0])

    return link


def wait(eng, sem, value):
    if not isinstance(value, int) or value > 0:
        eng.wait_ge(sem, value)


def pipelined(eng, n, front, step):
    front(0)
    step(0, True)
    with eng.Fori(1, n - 1) as t:
        step(t, True)
    step(n - 1, False)


def nothing(*_):
    pass


def root(pool, v, powers, out, eps_added, done, count):
    pool.tensor_tensor(v, v, powers[:, 0:1].broadcast_to(v.shape), ALU.add).then_inc(eps_added, 1)
    pool.wait_ge(eps_added, count)
    pool.tensor_tensor(out, v, powers[:, 1:2].broadcast_to(v.shape), ALU.pow).then_inc(done, 1)
def mamba2(nc, signals, x_in, x_out, w_x, w_bc, w_gate, w_out, conv, a_log, dt_bias, d_skip, norm_w, fill):
    T = 256
    B = 2
    C = T // P
    NT = x_in.shape[0] // (B * C)
    NS = NT * B
    DI = w_x.shape[1]
    M = DI // P
    H = a_log.shape[0]
    HD = DI // H
    N = 16
    HG = P // N
    G = H // HG
    GW = DI // G
    Q = 4
    HQ = H // Q
    LIMIT = 80.0
    with ExitStack() as ctx:
        def ps(name, shape):
            return ctx.enter_context(nc.psum_tensor(name, shape, F32))[:]

        def sem(name):
            return signals("a_" + name)

        sb = Sbuf(nc, SBUF_START, SBUF_END)
        ident = sb("a_ident", [P, P], F32)
        LOW = 32
        pick = sb("a_pick", [LOW + H, H], F32R)
        spread_h = sb("a_spread_h", [H, G, HG, N], F32)
        spread_n = sb("a_spread_n", [N, HG, N], F32)
        ident4 = sb("a_ident4", [P, HQ, P], mybir.dt.bfloat16)
        mask = sb("a_mask", [P, GW], mybir.dt.bfloat16)
        zeros = sb("a_zeros", [P, P], F32)
        cvec = sb("a_cvec", [P, M + 1, 5], F32)
        nega = sb("a_nega", [H, 1], F32)
        dtb = sb("a_dtb", [H, 1], F32)
        dsk = sb("a_dsk", [P, H], F32)
        nrm = sb("a_nrm", [P, M], F32)
        powers = sb("a_powers", [P, 2], F32)
        hold = sb("a_hold", [P, 1], F32)
        stats = sb("a_stats", [P, C, 6], F32)
        mv = sb("a_mv", [P, C, 4], F32)
        ssq = sb("a_ssq", [P, C, 2], F32)
        et = sb("a_et", [P, B, G, C], F32)
        carry = sb("a_carry", [P, B, M + 1, 3], F32)
        zero3 = sb("a_zero3", [P, 3], F32)
        wx = (sb("a_wxh", [P, KD, DI], F32R), sb("a_wxl", [P, KD, DI], F32R))
        wb = (sb("a_wbh", [P, KD, P], F32R), sb("a_wbl", [P, KD, P], F32R))
        wg = (sb("a_wgh", [P, KD, DI], F32R), sb("a_wgl", [P, KD, DI], F32R))
        wo = (sb("a_woh", [P, M, D], F32R), sb("a_wol", [P, M, D], F32R))
        xth = sb("a_xth", [P, B, KD, T], F32R)
        xtl = sb("a_xtl", [P, B, KD, T], F32R)
        da = sb("a_da", [LOW + H, B, T], F32R)
        dah, dal = da[0:H], da[LOW:LOW + H]
        ygh = sb("a_ygh", [P, M, P], F32R)
        ygl = sb("a_ygl", [P, M, P], F32R)
        at_work = sb.at
        xf = sb("a_xf", [P, C, D], F32)
        xr = sb("a_xr", [P, C, D], F32)
        pb = sb("a_pb", [64, T + 3], F32)
        xpre = sb("a_xpre", [P, 2, T + 3], F32)
        xs = sb("a_xs", [P, 2, T], F32)
        xtok = sb("a_xtok", [P, B, C, DI], F32)
        xdt = sb("a_xdt", [P, DI], F32)
        sg = sb("a_sg", [P, DI], F32)
        L = sb("a_L", [P, H, P], F32)
        yg = sb("a_yg", [P, DI], F32)
        S = sb("a_S", [P, B, G, GW], F32)
        bcs = sb("a_bcs", [P, B, T], F32)
        cs = sb("a_cs", [N, B, T], F32)
        ex = sb("a_ex", [P, B, G, T], F32)
        tmp = sb("a_tmp", [P, GW], F32)
        btok = sb("a_btok", [P, C, P], F32)
        gs = sb("a_gs", [P, P], F32)
        bw = sb("a_bw", [P, H, N], F32)
        z = sb("a_z", [H, T], F32)
        e = sb("a_e", [H, T], F32)
        u = sb("a_u", [H, T], F32)
        l = sb("a_l", [H, T], F32)
        one = sb("a_one", [H, T], mybir.dt.bfloat16)
        stage = Sbuf(nc, at_work, sb.at)("a_stage", [P, 4, 2 * D], F32)

        ps_t = ps("a_pst", [P, 2, KD, P])
        ps_r = ps("a_psr", [P, 2, D])
        ps_m = ps("a_psm", [P, D])
        ps_d = ps("a_psd", [P, HQ, P])
        ps_y = ps("a_psy", [P, G, GW])

        s_small, s_const, s_prep = sem("small"), sem("const"), sem("prep")
        s_stage = [sem(f"stage{i}") for i in range(4)]
        s_whi, s_wlo = sem("whi"), sem("wlo")
        s_x = [sem(f"x{j}") for j in range(C)]
        s_xr = [sem(f"xr{j}") for j in range(C)]
        s_st = [sem(f"st{j}") for j in range(C)]
        s_xt, s_xh, s_xl = sem("xt"), sem("xh"), sem("xl")
        s_bp, s_mb, s_bedge, s_bkeep, s_bacc, s_bchain, s_bc = (sem(n) for n in ("bp", "mb", "bedge", "bkeep", "bacc", "bchain", "bc"))
        s_bs, s_cs, s_bchain2 = sem("bs"), sem("cs"), sem("bchain2")
        s_dt, s_dta, s_dtr, s_dah, s_dal = sem("dt"), sem("dta"), sem("dtr"), sem("dah"), sem("dal")
        s_xp, s_pre, s_acc, s_edge, s_keep, s_xchain, s_xc, s_xs, s_xtr, s_xtok = (
            sem(n) for n in ("xp", "pre", "acc", "edge", "keep", "xchain", "xc", "xs", "xtr", "xtok"))
        s_gp, s_gs, s_dp, s_sc, s_bw, s_m, s_gate, s_sg = (sem(n) for n in ("gp", "gs", "dp", "sc", "bw", "m", "gate", "sg"))
        s_xdt, s_dx, s_yp, s_stp, s_stm, s_su, s_ga, s_yg, s_sq, s_rs = (
            sem(n) for n in ("xdt", "dx", "yp", "stp", "stm", "su", "ga", "yg", "sq", "rs"))
        s_yt, s_yh, s_yl, s_op, s_res, s_var, s_std, s_ln, s_ze, s_oe, s_bn = (
            sem(n) for n in ("yt", "yh", "yl", "op", "res", "var", "std", "ln", "ze", "oe", "bn"))
        s_dr, s_ec, s_et, s_cr, s_cx, s_btp, s_bt = (sem(n) for n in ("dr", "ec", "et", "cr", "cx", "btp", "bt"))

        pieces = [(w_bc.rearrange("(k p) n -> p k n", p=P), wb[0], wb[1], KD, None)]
        for w_dram, w in ((w_x, wx), (w_gate, wg)):
            for k in range(KD):
                pieces.append((w_dram[k * P:(k + 1) * P, :], w[0][:, k, :], w[1][:, k, :], 1, None))
        for m in range(0, M, 2):
            pieces.append((w_out[m * P:(m + 2) * P, :].rearrange("(a p) n -> p a n", p=P), wo[0][:, m:m + 2, :], wo[1][:, m:m + 2, :], 2, m))

        def staged(i):
            w, a = pieces[i][1], pieces[i][3]
            if a == 1:
                return stage[:, i % 4, :]
            return stage[:, i % 4, 0:a * w.shape[2]].rearrange("p (a n) -> p a n", a=a)

        def chunk(dram, t, b, j):
            return dram[bass.ds(t * C + (b * NT * C + j), 1), :, :].rearrange("a p d -> p (a d)")

        def before(t, b, n=1):
            b -= n
            while b < 0:
                t, b = t - 1, b + B
            return t, b

        def steps(eng, turn=nothing, lead=nothing, front=nothing, ssm=nothing, soft=nothing, rest=nothing, x_part=nothing,
                  z_part=nothing, o_part=nothing):
            def step(t, b):
                prev = before(t, b)
                has_prev = not isinstance(t, int) or t * B + b > 0
                turn(t, b)
                if has_prev:
                    lead(*prev, 0)
                front(t, b)
                if has_prev:
                    ssm(*prev, 0, lambda i: soft(t, b, i))
                else:
                    soft(t, b, 0)
                    soft(t, b, 1)
                x_part(t, b, 0, (lambda: lead(*prev, 1)) if has_prev else nothing)
                if has_prev:
                    z_part(*prev, 0)
                    ssm(*prev, 1, lambda i: soft(t, b, 2) if i == 0 else None)
                else:
                    soft(t, b, 2)

                def fill():
                    soft(t, b, 3)
                    if has_prev:
                        for i in range(3):
                            o_part(*prev, 0, i)

                x_part(t, b, 1, fill)
                if has_prev:
                    z_part(*prev, 1)
                rest(t, b, (lambda i: o_part(*prev, 1, i)) if has_prev else nothing)

            for b in range(B):
                step(0, b)
            with eng.Fori(1, NT) as t:
                for b in range(B):
                    step(t, b)
            end = (NT - 1, B - 1)
            for j in range(C):
                lead(*end, j)
                ssm(*end, j, nothing)
                z_part(*end, j)
                for i in range(3):
                    o_part(*end, j, i)

        block = ctx.enter_context(nc.Block())

        @block.sync
        def _(sp):
            for dst, src in ((cvec, conv), (nega, a_log.rearrange("(h a) -> h a", a=1)), (dtb, dt_bias.rearrange("(h a) -> h a", a=1)),
                             (dsk, d_skip.partition_broadcast(P)), (nrm, norm_w)):
                sp.dma_start(dst, src).then_inc(s_small, 16)
            for i, piece in enumerate(pieces):
                if i >= 4:
                    sp.wait_ge(s_wlo, i - 3)
                sp.dma_start(staged(i), piece[0]).then_inc(s_stage[i % 4], 16)
            sp.wait_ge(s_wlo, len(pieces))

            def store(t, b):
                s = B * t + b
                for j in range(C):
                    sp.wait_ge(s_ln, C * s + j + 1)
                    sp.dma_start(chunk(x_out, t, b, j), xr[:, j, :]).then_inc(s_st[j], 16)

            def load_r(t, b):
                s = B * t + b
                for j in range(C):
                    wait(sp, s_st[j], 16 * s)
                    sp.dma_start(xr[:, j, :], chunk(x_in, t, b, j)).then_inc(s_xr[j], 16)

            def step(t, b):
                s = B * t + b
                for j in range(C):
                    wait(sp, s_xt, C * (s - 1) + j + 1)
                    sp.dma_start(xf[:, j, :], chunk(x_in, t, b, j)).then_inc(s_x[j], 16)
                if not isinstance(t, int) or s > 1:
                    store(*before(t, b, 2))
                if not isinstance(t, int) or s > 0:
                    load_r(*before(t, b))

            for b in range(B):
                step(0, b)
            with sp.Fori(1, NT) as t:
                for b in range(B):
                    step(t, b)
            store(NT - 1, 0)
            load_r(NT - 1, 1)
            store(NT - 1, 1)
            for j in range(C):
                sp.wait_ge(s_st[j], 16 * NS)

        @block.gpsimd
        def _(pool):
            fill(pool, ident, s_const)
            pool.memset(powers[:, 0:1], EPS)
            pool.memset(powers[:, 1:2], -0.5).then_inc(s_const, 1)
            pool.memset(zero3, 0.0).then_inc(s_const, 1)
            pool.memset(zeros, 0.0).then_inc(s_const, 1)
            pool.memset(pick.bitcast(F32), 0.0).then_inc(s_const, 1)
            pool.memset(da.bitcast(F32), 0.0).then_inc(s_const, 1)
            pool.wait_ge(s_const, 7)
            for h in range(HQ):
                pool.tensor_copy(ident4[:, h, :], ident).then_inc(s_const, 1)
            for i, row in enumerate((0, LOW)):
                pool.wait_ge(s_const, 7 + HQ + i)
                pool.tensor_copy(pick[row:row + H, :], ident[row:row + H, row:row + H]).then_inc(s_const, 1)
            for g in range(G):
                pool.tensor_copy(spread_h[:, g], ident[0:H, g * HG:(g + 1) * HG].unsqueeze(2).broadcast_to([H, HG, N])).then_inc(s_const, 1)
            pool.tensor_copy(spread_n, ident[0:N, 0:N].unsqueeze(1).broadcast_to([N, HG, N])).then_inc(s_const, 1)
            heads = mask.rearrange("r (h p) -> r h p", h=HG)
            pool.wait_ge(s_const, 12 + HQ)
            pool.memset(mask, 1.0).then_inc(s_const, 1)
            pool.wait_ge(s_const, 13 + HQ)
            pool.affine_select(out=heads, in_=heads, compare_op=ALU.is_ge, fill=0.0, base=0,
                               pattern=[[-N, HG], [0, HD]], channel_multiplier=1).then_inc(s_const, 1)
            pool.wait_ge(s_const, 14 + HQ)
            pool.affine_select(out=heads, in_=heads, compare_op=ALU.is_ge, fill=0.0, base=N - 1,
                               pattern=[[N, HG], [0, HD]], channel_multiplier=-1).then_inc(s_const, 1)
            pool.wait_ge(s_wlo, len(pieces))
            pool.memset(S, 0.0).then_inc(s_const, 1)
            pool.memset(bcs, 0.0).then_inc(s_const, 1)
            pool.wait_ge(s_small, 80)
            pool.wait_ge(s_const, 17 + HQ)

            def front(t, b):
                s = B * t + b
                wait(pool, s_bc, s)
                wait(pool, s_bkeep, s)
                if isinstance(t, int):
                    pool.memset(pb[:, 0:3], 0.0).then_inc(s_bedge, 1)
                else:
                    pool.tensor_tensor(pb[:, 0:3], carry[0:64, b, M], zero3[0:64], ALU.add).then_inc(s_bedge, 1)
                pool.wait_ge(s_bedge, s + 1)
                pool.wait_ge(s_mb, 2 * s + 1)
                pool.tensor_tensor(carry[0:64, b, M], pb[:, T:T + 3], zero3[0:64], ALU.add).then_inc(s_bkeep, 1)

            def x_part(t, b, half, fill):
                s = B * t + b
                for m in range(4 * half, 4 * half + 4):
                    n = M * s + m
                    wait(pool, s_xc, n - 1)
                    wait(pool, s_keep, n)
                    if isinstance(t, int):
                        pool.memset(xpre[:, m % 2, 0:3], 0.0).then_inc(s_edge, 1)
                    else:
                        pool.tensor_tensor(xpre[:, m % 2, 0:3], carry[:, b, m], zero3, ALU.add).then_inc(s_edge, 1)
                    pool.wait_ge(s_edge, n + 1)
                    pool.wait_ge(s_pre, n + 1)
                    pool.tensor_tensor(carry[:, b, m], xpre[:, m % 2, T:T + 3], zero3, ALU.add).then_inc(s_keep, 1)
                fill()

            def ssm(t, b, j, between):
                n = C * (B * t + b) + j
                pool.wait_ge(s_xdt, n + 1)
                xj = xtok[:, b, j, :].rearrange("p (h d) -> p h d", h=H)
                pool.tensor_tensor(xj, xj, dsk.unsqueeze(2).broadcast_to([P, H, HD]), ALU.mult).then_inc(s_dx, 1)

            def z_part(t, b, j):
                n = C * (B * t + b) + j
                pool.wait_ge(s_sq, n + 1)
                root(pool, ssq[:, j, 0:1], powers, ssq[:, j, 1:2], s_ze, s_rs, n + 1)

            def o_part(t, b, j, third):
                if third == 0:
                    n = C * (B * t + b) + j
                    pool.wait_ge(s_var, n + 1)
                    root(pool, mv[:, j, 1:2], powers, mv[:, j, 2:3], s_oe, s_std, n + 1)

            def rest(t, b, fill):
                fill(0)

            steps(pool, front=front, ssm=ssm, rest=rest, x_part=x_part, z_part=z_part, o_part=o_part)

        @block.scalar
        def _(act):
            act.wait_ge(s_small, 80)
            for i, (_, hi, _, _, m) in enumerate(pieces):
                act.wait_ge(s_stage[i % 4], 16 * (i // 4 + 1))
                if m is None:
                    act.activation(hi, staged(i), ACT.Copy).then_inc(s_whi, 1)
                else:
                    act.activation(hi[:, 0, :], staged(i)[:, 0, :], ACT.Copy, scale=nrm[:, m:m + 1])
                    act.activation(hi[:, 1, :], staged(i)[:, 1, :], ACT.Copy, scale=nrm[:, m + 1:m + 2]).then_inc(s_whi, 1)
            act.wait_ge(s_prep, 1)
            act.activation(nega, nega, ACT.Exp).then_inc(s_prep, 1)
            act.wait_ge(s_prep, 3)
            act.wait_ge(s_const, 17 + HQ)
            act.wait_ge(s_wlo, len(pieces))

            def turn(t, b):
                s = B * t + b
                for j in range(C):
                    act.wait_ge(s_xt, C * s + j + 1)
                    act.activation(xth[:, b, :, j * P:(j + 1) * P], ps_t[:, j, :, :], ACT.Copy).then_inc(s_xh, 1)

            def lead(t, b, j):
                n = C * (B * t + b) + j
                act.wait_ge(s_gp, n + 1)
                wait(act, s_m, Q * n)
                act.activation(gs, ps_m[:, 0:P], ACT.Copy).then_inc(s_gs, 1)

            def front(t, b):
                s = B * t + b
                act.wait_ge(s_bp, s + 1)
                wait(act, s_bc, s)
                wait(act, s_bkeep, s)
                act.activation(pb[:, 3:T + 3], ps_m[0:64, 0:T], ACT.Copy).then_inc(s_mb, 1)
                act.activation(z, ps_m[64:64 + H, 0:T], ACT.Copy).then_inc(s_mb, 1)
                act.wait_ge(s_mb, 2 * s + 1)
                act.activation(bcs[0:64, b, :], pb[:, 3:T + 3], ACT.Identity, bias=cvec[0:64, M, 4:5],
                               scale=cvec[0:64, M, 3:4]).then_inc(s_bacc, 1)

            def soft(t, b, part):
                s = B * t + b
                if part == 0:
                    act.wait_ge(s_dt, 9 * s + 2)
                    act.activation(e, e, ACT.Exp).then_inc(s_dta, 1)
                    act.wait_ge(s_dt, 9 * s + 3)
                    act.activation(l, u, ACT.Ln).then_inc(s_dta, 1)
                if part == 2:
                    act.wait_ge(s_dt, 9 * s + 9)
                    act.activation(bcs[64:64 + H, b, :], z, ACT.Copy).then_inc(s_dtr, 1)
                    act.activation(e, z, ACT.Exp, scale=nega).then_inc(s_dta, 1)
                    act.wait_ge(s_dta, 3 * s + 3)
                    act.activation(dah[:, b, :], e, ACT.Copy).then_inc(s_dah, 1)
                    act.wait_ge(s_bc, s + 1)
                    act.activation(bcs[0:64, b, :], bcs[0:64, b, :], ACT.Silu).then_inc(s_bs, 1)
                    act.wait_ge(s_bs, s + 1)
                    act.activation(cs[:, b, :], bcs[32:32 + N, b, :], ACT.Copy).then_inc(s_cs, 1)

            def ssm(t, b, j, between):
                n = C * (B * t + b) + j
                for g in range(G):
                    act.wait_ge(s_gate, G * n + g + 1)
                    wait(act, s_yg, G * (n - 1) + g + 1)
                    act.activation(sg[:, g * GW:(g + 1) * GW], ps_r[:, g, :], ACT.Silu).then_inc(s_sg, 1)
                between(0)

            def x_part(t, b, half, fill):
                s = B * t + b
                base = 4 * half
                for i in range(6):
                    if i < 4:
                        m = base + i
                        n = M * s + m
                        act.wait_ge(s_xp, n + 1)
                        wait(act, s_xc, n - 1)
                        wait(act, s_keep, n - 1)
                        act.activation(xpre[:, m % 2, 3:T + 3], ps_r[:, m % 2, 0:T], ACT.Copy).then_inc(s_pre, 1)
                        act.wait_ge(s_pre, n + 1)
                        wait(act, s_xtr, n - 1)
                        act.activation(xs[:, m % 2, :], xpre[:, m % 2, 3:T + 3], ACT.Identity, bias=cvec[:, m, 4:5],
                                       scale=cvec[:, m, 3:4]).then_inc(s_acc, 1)
                    if 1 <= i < 5:
                        m = base + i - 1
                        act.wait_ge(s_xc, M * s + m + 1)
                        act.activation(xs[:, m % 2, :], xs[:, m % 2, :], ACT.Silu).then_inc(s_xs, 1)
                    if i == 4:
                        fill()
                    if i >= 2:
                        m = base + i - 2
                        act.wait_ge(s_xtr, M * s + m + 1)
                        act.activation(xtok[:, b, :, m * P:(m + 1) * P], ps_t[:, m % 2, 0:C, :], ACT.Copy).then_inc(s_xtok, 1)

            def z_part(t, b, j):
                n = C * (B * t + b) + j
                for q in range(2):
                    act.wait_ge(s_yt, 2 * n + q + 1)
                    act.activation(ygh[:, 4 * q:4 * q + 4, :], ps_t[:, q, :, :], ACT.Copy).then_inc(s_yh, 1)
                act.wait_ge(s_yg, G * n + G)
                act.activation(xtok[:, b, j, :], yg, ACT.Square, scale=DI ** -0.5, accum_out=ssq[:, j, 0:1]).then_inc(s_sq, 1)

            def rest(t, b, fill):
                s = B * t + b
                act.wait_ge(s_btp, s + 1)
                wait(act, s_m, Q * C * s)
                act.activation(btok, ps_m[:, 0:C * P].rearrange("p (j n) -> p j n", j=C), ACT.Copy).then_inc(s_bt, 1)

            steps(act, turn=turn, lead=lead, front=front, ssm=ssm, soft=soft, rest=rest, x_part=x_part, z_part=z_part)

        @block.vector
        def _(dve):
            dve.wait_ge(s_small, 80)
            for i, (_, hi, lo, _, m) in enumerate(pieces):
                dve.wait_ge(s_whi, i + 1)
                if m is None:
                    dve.tensor_tensor(lo, staged(i), hi.bitcast(F32), ALU.subtract).then_inc(s_wlo, 1)
                else:
                    for a in range(2):
                        ins = dve.scalar_tensor_tensor(out=lo[:, a, :], in0=staged(i)[:, a, :], scalar=nrm[:, m + a:m + a + 1],
                                                       in1=hi[:, a, :].bitcast(F32), op0=ALU.mult, op1=ALU.subtract)
                    ins.then_inc(s_wlo, 1)
            dve.tensor_scalar(nega, nega, LIMIT, None, ALU.min).then_inc(s_prep, 1)
            dve.wait_ge(s_prep, 2)
            dve.tensor_scalar(nega, nega, -1.0, None, ALU.mult).then_inc(s_prep, 1)
            dve.wait_ge(s_const, 17 + HQ)

            def taps(dst, src, vec, link_sem, base, done):
                for k in range(3):
                    ins = dve.scalar_tensor_tensor(out=dst, in0=src[:, k:k + T], scalar=vec[:, k:k + 1], in1=dst, op0=ALU.mult, op1=ALU.add)
                    if k < 2:
                        ins.then_inc(link_sem, 1)
                        dve.wait_ge(link_sem, base + k + 1)
                ins.then_inc(done, 1)

            def turn(t, b):
                s = B * t + b
                for j in range(C):
                    dve.wait_ge(s_xh, C * s + j + 1)
                    cols = slice(j * P, (j + 1) * P)
                    dve.tensor_tensor(xtl[:, b, :, cols], ps_t[:, j, :, :], xth[:, b, :, cols].bitcast(F32), ALU.subtract).then_inc(s_xl, 1)

            def scan(n, q):
                hq = slice(q * HQ, (q + 1) * HQ)
                dve.wait_ge(s_dp, Q * n + q + 1)
                if q == 0:
                    wait(dve, s_yp, G * n)
                dve.tensor_tensor_scan(L[:, hq, :].rearrange("p h t -> p (h t)"), ps_d.rearrange("p h t -> p (h t)"),
                                       ident4.rearrange("p h t -> p (h t)"), 0.0, ALU.mult, ALU.add).then_inc(s_sc, 1)

            def lead(t, b, j):
                n = C * (B * t + b) + j
                heads = "p (h d) -> p h d"
                dve.wait_ge(s_bt, B * t + b + 1)
                dve.wait_ge(s_xtok, M * (B * t + b) + M)
                wait(dve, s_stp, G * n)
                dve.tensor_tensor(xdt.rearrange(heads, h=H), xtok[:, b, j, :].rearrange(heads, h=H),
                                  btok[:, j, 64:64 + H].unsqueeze(2).broadcast_to([P, H, HD]), ALU.mult).then_inc(s_xdt, 1)
                scan(n, 0)

            def soft(t, b, part):
                s = B * t + b
                if part == 0:
                    dve.wait_ge(s_bacc, s + 1)
                    dve.wait_ge(s_bedge, s + 1)
                    taps(bcs[0:64, b, :], pb, cvec[0:64, M, :], s_bchain, 2 * s, s_bc)
                    link = chain(dve, s_dt, 9 * s)
                    dve.wait_ge(s_mb, 2 * s + 2)
                    link(dve.tensor_scalar(z, z, dtb, None, ALU.add))
                    wait(dve, s_dr, s)
                    wait(dve, s_dah, s)
                    link(dve.scalar_tensor_tensor(out=e, in0=z, scalar=-1.0, in1=z, op0=ALU.mult, op1=ALU.min))
                if part == 1:
                    dve.wait_ge(s_dta, 3 * s + 1)
                    dve.tensor_scalar(u, e, 1.0, None, ALU.add).then_inc(s_dt, 1)
                    dve.wait_ge(s_dt, 9 * s + 3)
                    dve.tensor_scalar(one, u, 1.0, None, ALU.is_equal).then_inc(s_dt, 1)
                if part == 2:
                    dve.wait_ge(s_dta, 3 * s + 2)
                    dve.wait_ge(s_dt, 9 * s + 4)
                    dve.scalar_tensor_tensor(out=u, in0=u, scalar=-1.0, in1=one, op0=ALU.add, op1=ALU.add).then_inc(s_dt, 1)
                    dve.wait_ge(s_dt, 9 * s + 5)
                    dve.reciprocal(u, u).then_inc(s_dt, 1)
                    dve.wait_ge(s_dt, 9 * s + 6)
                    dve.tensor_tensor(l, l, u, ALU.mult).then_inc(s_dt, 1)
                    dve.wait_ge(s_dt, 9 * s + 7)
                    dve.scalar_tensor_tensor(out=l, in0=l, scalar=1.0, in1=one, op0=ALU.mult, op1=ALU.add).then_inc(s_dt, 1)
                    dve.wait_ge(s_dt, 9 * s + 8)
                    dve.tensor_tensor(l, l, e, ALU.mult).then_inc(s_bchain2, 1)
                    dve.wait_ge(s_bchain2, s + 1)
                    dve.scalar_tensor_tensor(out=z, in0=z, scalar=0.0, in1=l, op0=ALU.max, op1=ALU.add).then_inc(s_dt, 1)
                if part == 3:
                    dve.wait_ge(s_dah, s + 1)
                    dve.tensor_tensor(dal[:, b, :], e, dah[:, b, :].bitcast(F32), ALU.subtract).then_inc(s_dal, 1)
                    dve.wait_ge(s_dal, 3 * s + 1)
                    for d in (dah, dal):
                        dve.memset(d.bitcast(F32)[:, b, :].rearrange("h (j n) -> h j n", j=C)[:, :, 0:1], 0.0).then_inc(s_dal, 1)

            def ssm(t, b, j, between):
                n = C * (B * t + b) + j
                for q in range(Q):
                    hq = slice(q * HQ, (q + 1) * HQ)
                    if q:
                        scan(n, q)
                    dve.wait_ge(s_sc, Q * n + q + 1)
                    dve.tensor_tensor(bw[:, hq, :], btok[:, j, 0:N].unsqueeze(1).broadcast_to([P, HQ, N]),
                                      L[:, hq, P - 1:P].broadcast_to([P, HQ, N]), ALU.mult).then_inc(s_bw, 1)
                    if q == 0:
                        dve.wait_ge(s_gs, n + 1)
                    dve.wait_ge(s_bw, Q * n + q + 1)
                    dve.tensor_tensor(L[:, hq, :], L[:, hq, :], gs.unsqueeze(1).broadcast_to([P, HQ, P]), ALU.mult).then_inc(s_m, 1)
                between(0)
                for g in range(G):
                    cols = slice(g * GW, (g + 1) * GW)
                    dve.wait_ge(s_stp, G * n + g + 1)
                    wait(dve, s_su, G * n + g)
                    dve.tensor_tensor(tmp, ps_m, mask, ALU.mult).then_inc(s_stm, 1)
                    dve.wait_ge(s_stm, G * n + g + 1)
                    dve.scalar_tensor_tensor(out=S[:, b, g, :], in0=S[:, b, g, :], scalar=et[:, b, g, j:j + 1], in1=tmp,
                                             op0=ALU.mult, op1=ALU.add).then_inc(s_su, 1)
                    dve.wait_ge(s_yp, G * n + g + 1)
                    dve.wait_ge(s_dx, n + 1)
                    wait(dve, s_yt, 2 * n)
                    wait(dve, s_sq, n)
                    dve.tensor_tensor(yg[:, cols], ps_y[:, g, :], xtok[:, b, j, cols], ALU.add).then_inc(s_ga, 1)
                    dve.wait_ge(s_ga, G * n + g + 1)
                    dve.wait_ge(s_sg, G * n + g + 1)
                    dve.tensor_tensor(yg[:, cols], yg[:, cols], sg[:, cols], ALU.mult).then_inc(s_yg, 1)
                    if g == 0:
                        between(1)

            def x_part(t, b, half, fill):
                s = B * t + b
                for m in range(4 * half, 4 * half + 4):
                    n = M * s + m
                    dve.wait_ge(s_edge, n + 1)
                    dve.wait_ge(s_acc, n + 1)
                    taps(xs[:, m % 2, :], xpre[:, m % 2, :], cvec[:, m, :], s_xchain, 2 * n, s_xc)
                fill()

            def z_part(t, b, j):
                n = C * (B * t + b) + j
                for q in range(2):
                    dve.wait_ge(s_yh, 2 * n + q + 1)
                    dve.tensor_tensor(ygl[:, 4 * q:4 * q + 4, :], ps_t[:, q, :, :], ygh[:, 4 * q:4 * q + 4, :].bitcast(F32),
                                      ALU.subtract).then_inc(s_yl, 1)

            def o_part(t, b, j, third):
                if third:
                    return
                s = B * t + b
                n = C * s + j
                out = xr[:, j, :]
                dve.wait_ge(s_rs, n + 1)
                dve.wait_ge(s_op, n + 1)
                dve.wait_ge(s_xr[j], 16 * s + 16)
                dve.scalar_tensor_tensor(out=out, in0=ps_r[:, 0, :], scalar=ssq[:, j, 1:2], in1=out, op0=ALU.mult, op1=ALU.add).then_inc(s_res, 1)
                dve.wait_ge(s_res, n + 1)
                dve.bn_stats(stats[:, j, :], out).then_inc(s_bn, 1)
                dve.wait_ge(s_bn, n + 1)
                dve.memset(hold, 0.0)
                dve.bn_aggr(mv[:, j, 0:2], stats[:, j, :]).then_inc(s_var, 1)
                dve.wait_ge(s_std, n + 1)
                dve.tensor_scalar(out, out, mv[:, j, 0:1], mv[:, j, 2:3], ALU.subtract, ALU.mult).then_inc(s_ln, 1)

            def rest(t, b, fill):
                s = B * t + b
                dve.wait_ge(s_dr, s + 1)
                for g in range(G):
                    for j in range(C):
                        cols = slice(j * P, (j + 1) * P)
                        dve.tensor_tensor_scan(ex[:, b, g, cols], ps_m[:, g * T + j * P:g * T + (j + 1) * P], zeros, 1.0,
                                               ALU.mult, ALU.add).then_inc(s_ec, 1)
                dve.wait_ge(s_ec, G * C * s + G * C)
                dve.tensor_copy(et[:, b], ex[:, b].rearrange("p g (j n) -> p g j n", j=C)[:, :, :, P - 1]).then_inc(s_et, 1)
                dve.wait_ge(s_et, s + 1)
                dve.wait_ge(s_cr, s + 1)
                dve.tensor_tensor(ex[:, b], ex[:, b], ps_m[:, 0:T].unsqueeze(1).broadcast_to([P, G, T]), ALU.mult).then_inc(s_cx, 1)
                fill(0)

            steps(dve, turn=turn, lead=lead, ssm=ssm, soft=soft, rest=rest, x_part=x_part, z_part=z_part, o_part=o_part)

        @block.tensor
        def _(pe):
            pe.wait_ge(s_const, 17 + HQ)

            def three(out, lhs, rhs, n, lo=0, hi=None):
                for k in range(lo, n if hi is None else hi):
                    for a, c in ((0, 0), (0, 1), (1, 0)):
                        last = pe.matmul(out, lhs(a, k), rhs(c, k), start=(k, a, c) == (0, 0, 0), stop=(k, a) == (n - 1, 1))
                return last

            def turn(t, b):
                s = B * t + b
                for j in range(C):
                    pe.wait_ge(s_x[j], 16 * s + 16)
                    wait(pe, s_yl, 4 * s - 5 + j)
                    wait(pe, s_xtok, M * (s - 1) + 6 + j + 1)
                    for k in range(KD):
                        last = pe.transpose(ps_t[:, j, k, :], xf[:, j, k * P:(k + 1) * P], ident)
                    last.then_inc(s_xt, 1)

            def front(t, b):
                s = B * t + b
                pe.wait_ge(s_xl, C * s + C)
                wait(pe, s_bt, s)
                wait(pe, s_gs, C * (s - 1) + 1)
                x = (xth, xtl)
                three(ps_m[:, 0:T], lambda a, k: wb[a][:, k, :], lambda c, k: x[c][:, b, k, :], KD).then_inc(s_bp, 1)

            def gate(t, b, j, g, free, lo=0, hi=KD):
                if lo == 0:
                    for f in free:
                        wait(pe, *f)
                x = (xth, xtl)
                last = three(ps_r[:, g, :], lambda a, k: x[a][:, b, k, j * P:(j + 1) * P],
                             lambda c, k: wg[c][:, k, g * GW:(g + 1) * GW], KD, lo, hi)
                if hi == KD:
                    last.then_inc(s_gate, 1)

            def decays(t, b, j, q):
                s = B * t + b
                pe.wait_ge(s_dal, 3 * s + 3)
                wait(pe, s_sc, Q * (C * s + j) + q)
                for h in range(HQ):
                    last = pe.matmul(ps_d[:, h, :], pick[:, q * HQ + h:q * HQ + h + 1].broadcast_to([LOW + H, P]),
                                     da[:, b, j * P:(j + 1) * P], start=True, stop=True)
                last.then_inc(s_dp, 1)

            def is_end(t, b):
                return isinstance(t, int) and B * t + b == NS - 1

            def lead(t, b, j):
                s = B * t + b
                cols = slice(j * P, (j + 1) * P)
                decays(t, b, j, 0)
                pe.wait_ge(s_cs, s + 1)
                pe.wait_ge(s_bt, s + 1)
                wait(pe, s_stm, G * (C * s + j))
                pe.matmul(ps_m[:, 0:P], bcs[0:N, b, cols], cs[:, b, cols], start=True, stop=True).then_inc(s_gp, 1)
                if j == 0:
                    free = [(s_pre, M * s + 7), (s_res, C * s)]
                elif not is_end(t, b):
                    free = [(s_pre, M * s + M + 3)]
                else:
                    free = [(s_sg, 4 * s + 1), (s_res, C * s + 1)]
                gate(t, b, j, 0, free)

            def ssm(t, b, j, between):
                s = B * t + b
                n = C * s + j
                cols = slice(j * P, (j + 1) * P)
                decays(t, b, j, 1)
                if j == 0:
                    free = [(s_pre, M * s + 8)]
                elif not is_end(t, b):
                    free = [(s_pre, M * s + M + 4)]
                else:
                    free = [(s_sg, 4 * s + 2)]
                gate(t, b, j, 1, free, 0, KD // 2)
                decays(t, b, j, 2)
                gate(t, b, j, 1, free, KD // 2, KD)
                decays(t, b, j, 3)
                pe.wait_ge(s_xdt, n + 1)
                pe.wait_ge(s_cx, s + 1)
                for g in range(G):
                    gc = slice(g * GW, (g + 1) * GW)
                    wait(pe, s_ga, G * (n - 1) + g + 1)
                    wait(pe, s_su, G * (n - 1) + g + 1)
                    pe.wait_ge(s_m, Q * n + (g + 1) * Q // G)
                    pe.matmul(ps_y[:, g, :], ex[:, b, g, cols], S[:, b, g, :], start=True, stop=False)
                    for h in range(g * HG, (g + 1) * HG):
                        o = (h - g * HG) * HD
                        last = pe.matmul(ps_y[:, g, o:o + HD], L[:, h, :], xdt[:, h * HD:(h + 1) * HD], start=False,
                                         stop=h == (g + 1) * HG - 1)
                    last.then_inc(s_yp, 1)
                    if g == 0:
                        pe.wait_ge(s_gs, n + 1)
                        if j == 0 and not is_end(t, b):
                            pe.wait_ge(s_mb, 2 * s + 4)
                    else:
                        pe.wait_ge(s_stm, G * n + g)
                    pe.matmul(ps_m[:, :], bw[:, g * HG:(g + 1) * HG, :].rearrange("p h n -> p (h n)"), xdt[:, gc], start=True, stop=True).then_inc(s_stp, 1)

            def x_part(t, b, half, fill):
                s = B * t + b
                x = (xth, xtl)
                base = 4 * half
                free = {0: [(s_sg, 4 * s - 3)], 1: [(s_sg, 4 * s - 2)], 2: [(s_pre, M * s + 1)], 3: [(s_pre, M * s + 2)],
                        4: [(s_sg, 4 * s - 1), (s_pre, M * s + 3)], 5: [(s_sg, 4 * s), (s_pre, M * s + 4)],
                        6: [(s_pre, M * s + 5)], 7: [(s_pre, M * s + 6)]}
                tfree = {0: [(s_xl, C * s + 1)], 1: [(s_xl, C * s + 2)], 2: [(s_xtok, M * s + 1)], 3: [(s_xtok, M * s + 2)],
                         4: [(s_yl, 4 * s - 3), (s_xtok, M * s + 3)], 5: [(s_yl, 4 * s - 2), (s_xtok, M * s + 4)],
                         6: [(s_xtok, M * s + 5)], 7: [(s_xtok, M * s + 6)]}
                for i in range(6):
                    if i < 4:
                        m = base + i
                        for f in free[m]:
                            wait(pe, *f)
                        three(ps_r[:, m % 2, 0:T], lambda a, k: wx[a][:, k, m * P:(m + 1) * P], lambda c, k: x[c][:, b, k, :],
                              KD).then_inc(s_xp, 1)
                    if i == 4:
                        fill()
                    if i >= 2:
                        m = base + i - 2
                        pe.wait_ge(s_xs, M * s + m + 1)
                        for f in tfree[m]:
                            wait(pe, *f)
                        for j in range(C):
                            last = pe.transpose(ps_t[:, m % 2, j, :], xs[:, m % 2, j * P:(j + 1) * P], ident)
                        last.then_inc(s_xtr, 1)

            def z_part(t, b, j):
                s = B * t + b
                n = C * s + j
                for q in range(2):
                    if not is_end(t, b):
                        pe.wait_ge(s_xtok, M * (s + 1) + 4 * j + 2 + q + 1)
                    else:
                        pe.wait_ge(s_yl, 2 * (n - 1) + q + 1)
                    pe.wait_ge(s_yg, G * n + q + 1)
                    for i in range(4):
                        last = pe.transpose(ps_t[:, q, i, :], yg[:, (4 * q + i) * P:(4 * q + i + 1) * P], ident)
                    last.then_inc(s_yt, 1)

            def o_part(t, b, j, third):
                s = B * t + b
                n = C * s + j
                if third == 0:
                    pe.wait_ge(s_yl, 2 * n + 2)
                    if is_end(t, b):
                        pe.wait_ge(s_sg, G * n + 1)
                    elif j == 0:
                        pe.wait_ge(s_pre, M * (s + 1) + 7)
                    else:
                        pe.wait_ge(s_res, n)
                y = (ygh, ygl)
                last = three(ps_r[:, 0, :], lambda a, k: y[a][:, k, :], lambda c, k: wo[c][:, k, :], M, 3 * third, min(3 * third + 3, M))
                if third == 2:
                    last.then_inc(s_op, 1)

            def rest(t, b, fill):
                s = B * t + b
                pe.wait_ge(s_dta, 3 * s + 3)
                pe.wait_ge(s_mb, 2 * s + 2)
                wait(pe, s_stm, 4 * s)
                for g in range(G):
                    last = pe.matmul(ps_m[:, g * T:(g + 1) * T], spread_h[:, g].rearrange("k h n -> k (h n)"), e,
                                     start=True, stop=True)
                last.then_inc(s_dr, 1)
                fill(0)
                pe.wait_ge(s_cs, s + 1)
                pe.wait_ge(s_ec, 4 * s + 4)
                pe.matmul(ps_m[:, 0:T], spread_n.rearrange("k h n -> k (h n)"), cs[:, b, :], start=True, stop=True).then_inc(s_cr, 1)
                fill(1)
                pe.wait_ge(s_dtr, s + 1)
                pe.wait_ge(s_cx, s + 1)
                for j in range(C):
                    last = pe.transpose(ps_m[:, j * P:(j + 1) * P], bcs[:, b, j * P:(j + 1) * P], ident)
                last.then_inc(s_btp, 1)
                fill(2)

            steps(pe, turn=turn, lead=lead, front=front, ssm=ssm, rest=rest, x_part=x_part, z_part=z_part, o_part=o_part)


def bounded_ffn(nc, signals, x_in, x_out, w, scale, fill, space, ahead, split):
    C = 4
    T = C * P
    NT = x_in.shape[0] // C
    TINY = 1e-7
    LIMIT = 0.99
    with ExitStack() as ctx:
        def ps(name, shape):
            return ctx.enter_context(nc.psum_tensor(name, shape, F32))[:]

        def sem(name):
            return signals(name)

        sb = Sbuf(nc, *space)
        ident = sb("b_ident", [P, P], F32)
        eps = sb("b_eps", [P, 1], F32)
        hold = sb("b_hold", [P, 1], F32)
        stats = sb("b_stats", [P, C, 6], F32)
        mv = sb("b_mv", [P, C, 2], F32)
        std = sb("b_std", [P, C], F32)
        ssq = sb("b_ssq", [P, C], F32)
        nrm = sb("b_nrm", [P, C], F32)
        nm = sb("b_nm", [P, C], F32)
        th = sb("b_th", [P, C], F32)
        f = sb("b_f", [P, C], F32)
        g = sb("b_g", [P, C], F32)
        scl = sb("b_scl", [P, D], F32)
        wh = sb("b_wh", [P, KD, D], F32R)
        wl = sb("b_wl", [P, KD, D], F32R)
        stage = sb("b_stage", [P, KD, D], F32)
        xth = sb("b_xth", [P, KD, T], F32R)
        xtl = sb("b_xtl", [P, KD, T], F32R)
        xin = sb("b_xin", [P, C, D], F32)
        res = sb("b_res", [P, C, D], F32)
        o = sb("b_o", [P, C, D], F32)
        sq = sb("b_sq", [P, C, D], F32)

        ps_t = ps("b_pst", [P, 2, KD, P])
        ps_o = ps("b_pso", [P, C, D])

        s_small = sem("b_small")
        s_const = sem("b_const")
        s_stage = sem("b_stage_in")
        s_whi = sem("b_whi")
        s_wlo = sem("b_wlo")
        s_x = [sem(f"b_x{c}") for c in range(C)]
        s_xt = sem("b_xt")
        s_xh = sem("b_xh")
        s_xl = sem("b_xl")
        s_mm = sem("b_mm")
        s_o = sem("b_o_done")
        s_ssq = sem("b_ssq_done")
        s_nrm = sem("b_nrm_done")
        s_th = sem("b_th_done")
        s_res = sem("b_res")
        s_next = sem("b_next")
        s_r = [sem(f"b_r{c}") for c in range(C)]
        s_bn = sem("b_bn")
        s_var = sem("b_var")
        s_std = sem("b_std_done")
        s_ln = sem("b_ln")
        s_chain = sem("b_chain")
        s_st = [sem(f"b_st{c}") for c in range(C)]

        def chunk(dram, t, c):
            return dram[bass.ds(t * C + c, 1), :, :].rearrange("a p d -> p (a d)")

        block = ctx.enter_context(nc.Block())

        @block.sync
        def _(sp):
            sp.dma_start(scl, scale.partition_broadcast(P)).then_inc(s_small, 16)

            def load_x(t):
                for c in range(C):
                    wait(sp, s_xt, C * (t - 1) + c + 1)
                    sp.dma_start(xin[:, c, :], chunk(x_in, t, c)).then_inc(s_x[c], 16)

            def load_r(t):
                for c in range(C):
                    wait(sp, s_res, C * (t - 1) + c + 1)
                    sp.dma_start(res[:, c, :], chunk(x_in, t, c)).then_inc(s_r[c], 16)

            load_x(0)
            sp.dma_start(stage, w.rearrange("(k p) n -> p k n", p=P)).then_inc(s_stage, 16)
            load_r(0)
            for dst, src, arrived in ahead:
                sp.dma_start(dst, src).then_inc(arrived, 16)

            def store(t):
                for c in range(C):
                    sp.wait_ge(s_ln, C * t + c + 1)
                    sp.dma_start(chunk(x_out, t, c), o[:, c, :]).then_inc(s_st[c], 16)

            def step(t, more):
                if more:
                    load_x(t + 1)
                    load_r(t + 1)
                store(t)

            pipelined(sp, NT, nothing, step)
            for c in range(C):
                sp.wait_ge(s_st[c], 16 * NT)

        @block.gpsimd
        def _(pool):
            fill(pool, ident, s_const)
            pool.memset(eps, EPS).then_inc(s_const, 1)
            for i, (raw, arrived, hi, lo) in enumerate(split):
                pool.wait_ge(arrived, 16)
                pool.tensor_copy(hi, raw).then_inc(s_next, 1)
                pool.wait_ge(s_next, 2 * i + 1)
                pool.tensor_tensor(lo, raw, hi.bitcast(F32), ALU.subtract).then_inc(s_next, 1)

        @block.scalar
        def _(act):
            act.wait_ge(s_const, 3)

            def front(t):
                for c in range(C):
                    act.wait_ge(s_xt, C * t + c + 1)
                    act.activation(xth[:, :, c * P:(c + 1) * P], ps_t[:, c % 2, :, :], ACT.Copy).then_inc(s_xh, 1)
                if isinstance(t, int) and t == 0:
                    act.wait_ge(s_stage, 16)
                    act.activation(wh, stage, ACT.Copy).then_inc(s_whi, 1)

            def step(t, more):
                for c in range(C):
                    act.wait_ge(s_o, C * t + c + 1)
                    act.activation(sq[:, c, :], o[:, c, :], ACT.Square, accum_out=ssq[:, c:c + 1]).then_inc(s_ssq, 1)
                if more:
                    front(t + 1)
                act.wait_ge(s_ssq, C * t + C)
                act.activation(nrm, ssq, ACT.Sqrt).then_inc(s_nrm, 1)
                act.wait_ge(s_nrm, 2 * t + 2)
                act.activation(th, nm, ACT.Tanh).then_inc(s_th, 1)
                act.wait_ge(s_var, C * t + C)
                act.activation(std, mv[:, :, 1], ACT.Sqrt, bias=eps).then_inc(s_std, 1)

            pipelined(act, NT, front, step)

        @block.vector
        def _(dve):

            def front(t):
                for c in range(C):
                    dve.wait_ge(s_xh, C * t + c + 1)
                    cols = slice(c * P, (c + 1) * P)
                    dve.tensor_tensor(xtl[:, :, cols], ps_t[:, c % 2, :, :], xth[:, :, cols].bitcast(F32), ALU.subtract).then_inc(s_xl, 1)
                if isinstance(t, int) and t == 0:
                    dve.wait_ge(s_whi, 1)
                    dve.tensor_tensor(wl, stage, wh.bitcast(F32), ALU.subtract).then_inc(s_wlo, 1)
                    dve.wait_ge(s_small, 16)

            def step(t, more):
                for c in range(C):
                    dve.wait_ge(s_mm, C * t + c + 1)
                    wait(dve, s_st[c], 16 * t)
                    dve.tensor_tensor(o[:, c, :], ps_o[:, c, :], scl, ALU.mult).then_inc(s_o, 1)
                if more:
                    front(t + 1)
                link = chain(dve, s_chain, 9 * t)
                dve.wait_ge(s_nrm, 2 * t + 1)
                dve.tensor_scalar(nm, nrm, TINY, None, ALU.max).then_inc(s_nrm, 1)
                dve.wait_ge(s_nrm, 2 * t + 2)
                link(dve.tensor_scalar(f, nm, TINY, None, ALU.add))
                link(dve.reciprocal(f, f))
                dve.wait_ge(s_th, t + 1)
                link(dve.tensor_tensor(f, f, th, ALU.mult))
                link(dve.tensor_tensor(g, f, nrm, ALU.mult))
                link(dve.tensor_scalar(g, g, TINY, None, ALU.max))
                link(dve.reciprocal(g, g))
                link(dve.tensor_scalar(g, g, LIMIT, 1.0, ALU.mult, ALU.min))
                link(dve.tensor_tensor(f, f, g, ALU.mult))
                for c in range(C):
                    dve.wait_ge(s_r[c], 16 * t + 16)
                    dve.scalar_tensor_tensor(out=o[:, c, :], in0=o[:, c, :], scalar=f[:, c:c + 1], in1=res[:, c, :],
                                             op0=ALU.mult, op1=ALU.add).then_inc(s_res, 1)
                for c in range(C):
                    dve.wait_ge(s_res, C * t + c + 1)
                    dve.bn_stats(stats[:, c, :], o[:, c, :]).then_inc(s_bn, 1)
                dve.wait_ge(s_bn, C * t + C)
                dve.memset(hold, 0.0)
                for c in range(C):
                    dve.bn_aggr(mv[:, c, :], stats[:, c, :]).then_inc(s_var, 1)
                dve.wait_ge(s_std, t + 1)
                link(dve.reciprocal(std, std))
                for c in range(C):
                    dve.tensor_scalar(o[:, c, :], o[:, c, :], mv[:, c, 0:1], std[:, c:c + 1], ALU.subtract, ALU.mult).then_inc(s_ln, 1)

            pipelined(dve, NT, front, step)

        @block.tensor
        def _(pe):
            pe.wait_ge(s_const, 3)

            def front(t):
                for c in range(C):
                    pe.wait_ge(s_x[c], 16 * t + 16)
                    wait(pe, s_xl, C * t + c - 1)
                    for k in range(KD):
                        last = pe.transpose(ps_t[:, c % 2, k, :], xin[:, c, k * P:(k + 1) * P], ident)
                    last.then_inc(s_xt, 1)

            def step(t, more):
                pe.wait_ge(s_wlo, 1)
                for c in range(C):
                    pe.wait_ge(s_xl, C * t + c + 1)
                    wait(pe, s_o, C * (t - 1) + c + 1)
                    i = 0
                    for k in range(KD):
                        for x, wp in ((xth, wh), (xth, wl), (xtl, wh)):
                            last = pe.matmul(ps_o[:, c, :], x[:, k, c * P:(c + 1) * P], wp[:, k, :], start=i == 0, stop=i == 3 * KD - 1)
                            i += 1
                    last.then_inc(s_mm, 1)
                if more:
                    front(t + 1)

            pipelined(pe, NT, front, step)


def rg_lru(nc, signals, x_in, x_out, vectors, b_out, fill, W, space, ahead):
    T = 256
    B = 2
    C = T // P
    NT = x_in.shape[0] // (B * C)
    M = KD
    with ExitStack() as ctx:
        def ps(name, shape):
            return ctx.enter_context(nc.psum_tensor(name, shape, F32))[:]

        def sem(name):
            return signals(name)

        sb = Sbuf(nc, *space)
        ident = sb("c_ident", [P, P], F32)
        vec = sb("c_vec", [P, 10, M], F32)
        BX, BY, BIG, BAG, CB, AP, W0 = range(7)
        spt = sb("c_spt", [P, 6, M], F32)
        powers = sb("c_powers", [P, 2], F32)
        hold = sb("c_hold", [P, 1], F32)
        stats = sb("c_stats", [P, C, 6], F32)
        mv = sb("c_mv", [P, C, 4], F32)
        bo = sb("c_bo", [P, D], F32)
        xth = sb("c_xth", [P, B, KD, T], F32R)
        xtl = sb("c_xtl", [P, B, KD, T], F32R)
        cvh = sb("c_cvh", [P, M, T], F32R)
        cvl = sb("c_cvl", [P, M, T], F32R)
        hyh = sb("c_hyh", [P, M, T], F32R)
        hyl = sb("c_hyl", [P, M, T], F32R)
        xin = sb("c_xin", [P, B * C, D], F32)
        xpre = sb("c_xpre", [P, M, T + 3], F32)
        carry = sb("c_carry", [P, B, M, 3], F32)
        zero3 = sb("c_zero3", [P, M, 3], F32)
        hlast = sb("c_hlast", [P, B, M, 1], F32)
        cv = sb("c_cv", [P, M, T], F32)
        y = sb("c_y", [P, B, M, T], F32)
        gx = sb("c_gx", [P, M, T], F32)
        a = sb("c_a", [P, M, T], F32)
        mu = sb("c_mu", [P, M, T], F32)
        hs = sb("c_hs", [P, M, T], F32)
        r = sb("c_r", [P, C, D], F32)

        ps_t = ps("c_pst", [P, C, KD, P])
        ps_a = ps("c_psa", [P, 2, 2, T])
        ps_b = ps("c_psb", [P, 2, 2, T])
        ps_o = ps("c_pso", [P, C, D])

        s_small = sem("c_small")
        s_const = sem("c_const")
        s_sp = sem("c_sp")
        s_sp_act = sem("c_sp_act")
        s_x = [sem(f"c_x{i}") for i in range(B * C)]
        s_xt = sem("c_xt")
        s_xh = sem("c_xh")
        s_xl = sem("c_xl")
        s_xb = sem("c_xb")
        s_pre = sem("c_pre")
        s_edge = sem("c_edge")
        s_keep = sem("c_keep")
        s_acc = sem("c_acc")
        s_conv = sem("c_conv")
        s_cvh = sem("c_cvh")
        s_cvl = sem("c_cvl")
        s_yp = sem("c_yp")
        s_y = sem("c_y")
        s_ig = sem("c_ig")
        s_ag = sem("c_ag")
        s_gx = sem("c_gx")
        s_ga = sem("c_ga")
        s_a = sem("c_a")
        s_a2 = sem("c_a2")
        s_gc = sem("c_gc")
        s_one = sem("c_one")
        s_mu = sem("c_mu")
        s_scan = sem("c_scan")
        s_hy = sem("c_hy")
        s_hyh = sem("c_hyh")
        s_hyl = sem("c_hyl")
        s_bo = sem("c_bo")
        s_out = sem("c_out")
        s_res = sem("c_res")
        s_var = sem("c_var")
        s_std = sem("c_std")
        s_ln = sem("c_ln")
        s_chain = sem("c_chain")
        s_hchain = sem("c_hchain")
        s_cchain = sem("c_cchain")
        s_eps = sem("c_eps")
        s_st = [sem(f"c_st{i}") for i in range(C)]
        s_r = [sem(f"c_r{i}") for i in range(C)]

        def chunk(dram, t, b, j):
            return dram[bass.ds(t * C + (b * NT * C + j), 1), :, :].rearrange("a p d -> p (a d)")

        def following(t, b):
            return (t, 1) if b == 0 else (t + 1, 0)

        def preceding(t, b):
            return (t, 0) if b else (t - 1, 1)

        def steps(eng, step, front=nothing, after=nothing):
            front(0, 0)
            for b in range(B):
                step(0, b, b == 0, True)
            with eng.Fori(1, NT - 1) as t:
                for b in range(B):
                    step(t, b, False, True)
            for b in range(B):
                step(NT - 1, b, False, b == 0)
            after()

        block = ctx.enter_context(nc.Block())

        @block.sync
        def _(sp):
            sp.dma_start(vec, vectors).then_inc(s_small, 16)
            sp.dma_start(bo, b_out.partition_broadcast(P)).then_inc(s_small, 16)

            def load_x(t, b):
                for j in range(C):
                    wait(sp, s_xt, C * (B * t + b - B) + j + 1)
                    sp.dma_start(xin[:, b * C + j, :], chunk(x_in, t, b, j)).then_inc(s_x[b * C + j], 16)

            def load_r(t, b):
                s = B * t + b
                for j in range(C):
                    wait(sp, s_st[j], 16 * s)
                    sp.dma_start(r[:, j, :], chunk(x_in, t, b, j)).then_inc(s_r[j], 16)

            def store(t, b):
                s = B * t + b
                for j in range(C):
                    sp.wait_ge(s_ln, C * s + j + 1)
                    sp.dma_start(chunk(x_out, t, b, j), r[:, j, :]).then_inc(s_st[j], 16)

            def step(t, b, first, more):
                if not (isinstance(t, int) and t == NT - 1):
                    load_x(t + 1, b)
                if not first:
                    store(*preceding(t, b))
                load_r(t, b)

            load_x(0, 0)
            load_x(0, 1)
            for dst, src, arrived in ahead:
                sp.dma_start(dst, src).then_inc(arrived, 16)
            steps(sp, step)
            store(NT - 1, B - 1)
            for j in range(C):
                sp.wait_ge(s_st[j], 16 * NT * B)

        @block.gpsimd
        def _(pool):
            fill(pool, ident, s_const)
            pool.memset(powers[:, 0:1], EPS)
            pool.memset(powers[:, 1:2], -0.5).then_inc(s_const, 1)
            pool.memset(zero3, 0.0).then_inc(s_const, 1)
            pool.memset(hlast, 0.0).then_inc(s_const, 1)
            pool.wait_ge(s_const, 5)
            pool.wait_ge(s_small, 32)

            def norm(t, b):
                s = B * t + b
                for j in range(C):
                    pool.wait_ge(s_var, C * s + j + 1)
                    root(pool, mv[:, j, 1:2], powers, mv[:, j, 2:3], s_eps, s_std, C * s + j + 1)

            def step(t, b, first, more):
                s = 2 * t + b
                wait(pool, s_conv, s)
                wait(pool, s_keep, s)
                if isinstance(t, int) and t == 0:
                    pool.memset(xpre[:, :, 0:3], 0.0).then_inc(s_edge, 1)
                else:
                    pool.tensor_tensor(xpre[:, :, 0:3], carry[:, b], zero3, ALU.add).then_inc(s_edge, 1)
                pool.wait_ge(s_edge, s + 1)
                pool.wait_ge(s_pre, M * s + M)
                pool.tensor_tensor(carry[:, b], xpre[:, :, T:T + 3], zero3, ALU.add).then_inc(s_keep, 1)
                if not first:
                    norm(*preceding(t, b))
                pool.wait_ge(s_gx, M * s + M)
                pool.tensor_tensor(gx, gx, cv, ALU.mult).then_inc(s_gc, 1)
                if isinstance(t, int) and t == 0:
                    wait(pool, s_hchain, s)
                    pool.memset(mu[:, :, 0:1], 1.0).then_inc(s_one, 1)
                for j in range(C):
                    pool.wait_ge(s_r[j], 16 * s + 16)
                    pool.tensor_tensor(r[:, j, :], r[:, j, :], bo, ALU.add).then_inc(s_bo, 1)

            steps(pool, step, after=lambda: norm(NT - 1, B - 1))

        @block.scalar
        def _(act):
            act.wait_ge(s_small, 32)
            act.wait_ge(s_const, 5)
            act.wait_ge(s_sp, 1)
            act.activation(spt[:, 0, :], spt[:, 0, :], ACT.Exp).then_inc(s_sp_act, 1)
            act.wait_ge(s_sp, 2)
            act.activation(spt[:, 2, :], spt[:, 1, :], ACT.Ln).then_inc(s_sp_act, 1)
            act.wait_ge(s_sp, 10)

            def high_hy(t, b):
                act.wait_ge(s_hy, 2 * t + b + 1)
                act.activation(hyh, hs, ACT.Copy).then_inc(s_hyh, 1)

            def front(t, b):
                for j in range(C):
                    act.wait_ge(s_xt, C * (B * t + b) + j + 1)
                    act.activation(xth[:, b, :, j * P:(j + 1) * P], ps_t[:, j, :, :], ACT.Copy).then_inc(s_xh, 1)

            def step(t, b, first, more):
                s = B * t + b
                wait(act, s_conv, s)
                wait(act, s_keep, s)
                for m in range(M):
                    act.wait_ge(s_xb, 2 * s + m // 2 + 1)
                    act.activation(xpre[:, m, 3:T + 3], ps_a[:, m // 2, m % 2, :], ACT.Identity,
                                   bias=vec[:, BX, m:m + 1]).then_inc(s_pre, 1)
                if not first:
                    high_hy(*preceding(t, b))
                wait(act, s_gc, s)
                act.wait_ge(s_pre, M * s + M)
                for m in range(M):
                    act.activation(cv[:, m, :], xpre[:, m, 3:T + 3], ACT.Identity, bias=vec[:, CB, m:m + 1],
                                   scale=vec[:, W0 + 3, m:m + 1]).then_inc(s_acc, 1)
                for m in range(M):
                    act.wait_ge(s_yp, 2 * s + m // 2 + 1)
                    wait(act, s_hy, s - 1)
                    act.activation(y[:, b, m, :], ps_b[:, m // 2, m % 2, :], ACT.Gelu, bias=vec[:, BY, m:m + 1]).then_inc(s_y, 1)
                act.wait_ge(s_conv, s + 1)
                act.activation(cvh, cv, ACT.Copy).then_inc(s_cvh, 1)
                if more:
                    front(*following(t, b))
                for m in range(M):
                    act.wait_ge(s_ig, 2 * s + m // 2 + 1)
                    wait(act, s_hy, s)
                    act.activation(gx[:, m, :], ps_a[:, m // 2, m % 2, :], ACT.Sigmoid, bias=vec[:, BIG, m:m + 1]).then_inc(s_gx, 1)
                for m in range(M):
                    act.wait_ge(s_ag, 2 * s + m // 2 + 1)
                    act.activation(a[:, m, :], ps_b[:, m // 2, m % 2, :], ACT.Sigmoid, bias=vec[:, BAG, m:m + 1]).then_inc(s_ga, 1)
                act.wait_ge(s_ga, M * s + M)
                for m in range(M):
                    act.activation(a[:, m, :], a[:, m, :], ACT.Exp, scale=spt[:, 5, m:m + 1]).then_inc(s_a, 1)
                act.wait_ge(s_a2, s + 1)
                left = mu[:, :, 1:T] if isinstance(t, int) and t == 0 else mu
                act.activation(left, left, ACT.Sqrt, scale=-1.0, bias=1.0).then_inc(s_mu, 1)

            steps(act, step, front, lambda: high_hy(NT - 1, B - 1))

        @block.vector
        def _(dve):
            dve.wait_ge(s_small, 32)
            dve.wait_ge(s_const, 5)
            z = vec[:, AP, :]
            e, u, l, one, q, scale = (spt[:, i, :] for i in range(6))
            link = chain(dve, s_sp, 0)
            link(dve.scalar_tensor_tensor(out=e, in0=z, scalar=-1.0, in1=z, op0=ALU.mult, op1=ALU.min))
            dve.wait_ge(s_sp_act, 1)
            link(dve.tensor_scalar(u, e, 1.0, None, ALU.add))
            dve.wait_ge(s_sp_act, 2)
            link(dve.tensor_scalar(one, u, 1.0, None, ALU.is_equal))
            link(dve.scalar_tensor_tensor(out=q, in0=u, scalar=-1.0, in1=one, op0=ALU.add, op1=ALU.add))
            link(dve.reciprocal(q, q))
            link(dve.tensor_tensor(q, q, l, ALU.mult))
            link(dve.tensor_tensor(q, q, one, ALU.add))
            link(dve.tensor_tensor(q, q, e, ALU.mult))
            link(dve.scalar_tensor_tensor(out=q, in0=z, scalar=0.0, in1=q, op0=ALU.max, op1=ALU.add))
            link(dve.tensor_scalar(scale, q, -8.0, None, ALU.mult))

            def recur(t, b):
                s = 2 * t + b
                dve.wait_ge(s_mu, s + 1)
                dve.wait_ge(s_gc, s + 1)
                dve.tensor_tensor(gx, gx, mu, ALU.mult).then_inc(s_hchain, 1)
                dve.wait_ge(s_hchain, s + 1)
                wait(dve, s_hyh, s)
                for m in range(M):
                    dve.tensor_tensor_scan(hs[:, m, :], a[:, m, :], gx[:, m, :],
                                           hlast[:, b, m, :],
                                           ALU.mult, ALU.add).then_inc(s_scan, 1)
                dve.wait_ge(s_scan, (M + 1) * s + M)
                dve.tensor_copy(hlast[:, b], hs[:, :, T - 1:T]).then_inc(s_scan, 1)
                dve.wait_ge(s_scan, (M + 1) * s + M + 1)
                dve.wait_ge(s_y, M * s + M)
                dve.tensor_tensor(hs, hs, y[:, b], ALU.mult).then_inc(s_hy, 1)
                dve.wait_ge(s_hyh, s + 1)
                dve.tensor_tensor(hyl, hs, hyh.bitcast(F32), ALU.subtract).then_inc(s_hyl, 1)

            def norm(t, b):
                s = 2 * t + b
                link = chain(dve, s_chain, C * s)
                for j in range(C):
                    out = r[:, j, :]
                    dve.wait_ge(s_out, C * s + j + 1)
                    dve.wait_ge(s_bo, C * s + j + 1)
                    dve.tensor_tensor(out, ps_o[:, j, :], out, ALU.add).then_inc(s_res, 1)
                    dve.wait_ge(s_res, C * s + j + 1)
                    link(dve.bn_stats(stats[:, j, :], out))
                    dve.memset(hold, 0.0)
                    dve.bn_aggr(mv[:, j, 0:2], stats[:, j, :]).then_inc(s_var, 1)
                for j in range(C):
                    out = r[:, j, :]
                    dve.wait_ge(s_std, C * s + j + 1)
                    dve.tensor_scalar(out, out, mv[:, j, 0:1], mv[:, j, 2:3], ALU.subtract, ALU.mult).then_inc(s_ln, 1)

            def front(t, b):
                s = B * t + b
                for j in range(C):
                    dve.wait_ge(s_xh, C * s + j + 1)
                    cols = slice(j * P, (j + 1) * P)
                    dve.tensor_tensor(xtl[:, b, :, cols], ps_t[:, j, :, :], xth[:, b, :, cols].bitcast(F32), ALU.subtract).then_inc(s_xl, 1)

            def step(t, b, first, more):
                s = B * t + b
                if not first:
                    recur(*preceding(t, b))
                dve.wait_ge(s_edge, s + 1)
                dve.wait_ge(s_acc, M * s + M)
                for k in range(3):
                    for m in range(M):
                        ins = dve.scalar_tensor_tensor(out=cv[:, m, :], in0=xpre[:, m, k:k + T], scalar=vec[:, W0 + k, m:m + 1],
                                                       in1=cv[:, m, :], op0=ALU.mult, op1=ALU.add)
                        if k < 2:
                            ins.then_inc(s_cchain, 1)
                        elif m == M - 1:
                            ins.then_inc(s_conv, 1)
                    if k < 2:
                        dve.wait_ge(s_cchain, 2 * M * s + M * (k + 1))
                dve.wait_ge(s_cvh, s + 1)
                dve.tensor_tensor(cvl, cv, cvh.bitcast(F32), ALU.subtract).then_inc(s_cvl, 1)
                if more:
                    front(*following(t, b))
                if not first:
                    norm(*preceding(t, b))
                dve.wait_ge(s_a, M * s + M)
                own = slice(1, T) if isinstance(t, int) and t == 0 else slice(0, T)
                if isinstance(t, int) and t == 0:
                    dve.wait_ge(s_one, s + 1)
                dve.tensor_tensor(mu[:, :, own], a[:, :, own], a[:, :, own], ALU.mult).then_inc(s_a2, 1)

            def last():
                recur(NT - 1, 1)
                norm(NT - 1, 1)

            steps(dve, step, front, last)

        @block.tensor
        def _(pe):
            pe.wait_ge(s_const, 5)

            def project(ps_x, w, xh, xl, free, done, low=None):
                for q in range(2):
                    free(q)
                    for m in (2 * q, 2 * q + 1):
                        i = 0
                        for wp, x in ((w[0], xh), (w[1], xh), (w[0], xl)):
                            if x is xl and low:
                                pe.wait_ge(*low)
                            for k in range(KD):
                                last = pe.matmul(ps_x[:, q, m % 2, :], wp[:, k, m * P:(m + 1) * P], x[:, k, :],
                                                 start=i == 0, stop=i == 3 * KD - 1)
                                i += 1
                    last.then_inc(done, 1)

            def output(t, b):
                s = 2 * t + b
                pe.wait_ge(s_hyl, s + 1)
                for j in range(C):
                    wait(pe, s_res, C * (s - 1) + j + 1)
                    i = 0
                    for k in range(KD):
                        for h, wp in ((hyh, W["out"][0]), (hyh, W["out"][1]), (hyl, W["out"][0])):
                            last = pe.matmul(ps_o[:, j, :], h[:, k, j * P:(j + 1) * P], wp[:, k, :], start=i == 0, stop=i == 3 * KD - 1)
                            i += 1
                    last.then_inc(s_out, 1)

            def front(t, b):
                s = B * t + b
                for j in range(C):
                    pe.wait_ge(s_x[b * C + j], 16 * t + 16)
                    wait(pe, s_xl, C * (s - 1) + j + 1)
                    for k in range(KD):
                        last = pe.transpose(ps_t[:, j, k, :], xin[:, b * C + j, k * P:(k + 1) * P], ident)
                    last.then_inc(s_xt, 1)

            def step(t, b, first, more):
                s = B * t + b
                pe.wait_ge(s_xl, C * s + C)
                project(ps_a, W["x"], xth[:, b], xtl[:, b], lambda q: wait(pe, s_gx, M * (s - 1) + 2 * q + 2), s_xb)
                project(ps_b, W["y"], xth[:, b], xtl[:, b], lambda q: wait(pe, s_ga, M * (s - 1) + 2 * q + 2), s_yp)
                if not first:
                    output(*preceding(t, b))
                if more:
                    front(*following(t, b))
                pe.wait_ge(s_cvh, s + 1)
                project(ps_a, W["ig"], cvh, cvl, lambda q: wait(pe, s_pre, M * s + 2 * q + 2), s_ig, (s_cvl, s + 1))
                project(ps_b, W["ag"], cvh, cvl, lambda q: wait(pe, s_y, M * s + 2 * q + 2), s_ag)

            steps(pe, step, front, lambda: output(NT - 1, B - 1))


ZERO_POINT = 128.0


def ffn_codes(nc, gate_wt, up_wt):
    ff = gate_wt.shape[1]
    start = SBUF_END - 4 * KD * (ff + ff // 2)
    sb = Sbuf(nc, start, SBUF_END)
    up = sb("d_wu_early_codes", [P, KD, ff // 2], I32)
    gate = sb("d_wg_codes", [P, KD, ff], I32)
    transfers = []
    for k in range(KD):
        transfers.append((gate[:, k, :], gate_wt[k * P:(k + 1) * P, :]))
        transfers.append((up[:, k, :], up_wt[k * P:(k + 1) * P, 0:ff // 2]))
    return (start, up, gate, 16 * len(transfers)), transfers


def gated_ffn(nc, signals, x_in, x_out, gate_wt, up_wt, down_wt, gate_scale, up_scale, down_scale, ident_fill, codes, s_codes):
    T = 512
    NT = x_in.shape[0] * P // T
    C = T // P
    FF = gate_wt.shape[1]
    M = FF // P
    with ExitStack() as ctx:
        def ps(name, shape):
            return ctx.enter_context(nc.psum_tensor(name, shape, F32))[:]

        def sem(name):
            return signals(name)

        sb = Sbuf(nc, SBUF_START, codes[0])
        ident = sb("d_ident", [P, P], F32)
        gs = sb("d_gs", [P, M], F32)
        us = sb("d_us", [P, M], F32)
        powers = sb("d_powers", [P, 2], F32)
        hold = sb("d_hold", [P, 1], F32)
        stats = sb("d_stats", [P, 2, 6], F32)
        mv = sb("d_mv", [P, 2, 4], F32)
        dsb = sb("d_dsb", [P, D], F32)
        half_ff = FF // 2
        late = sb.at
        wu_late = sb("d_wu_late", [P, KD, half_ff], F32R)
        wd = sb("d_wd", [P, M, D], F32R)
        sb_late = Sbuf(nc, late, sb.at)
        wu_late_codes = sb_late("d_wu_late_codes", [P, KD, half_ff], I32)
        wd_codes = sb_late("d_wd_codes", [P, M, D], I32)
        sb_early = Sbuf(nc, codes[0], SBUF_END)
        wu_early = sb_early("d_wu_early", [P, KD, half_ff], F32R)
        wg = sb_early("d_wg", [P, KD, FF], F32R)
        xth = sb("d_xth", [P, KD, T], F32R)
        xtl = sb("d_xtl", [P, KD, T], F32R)
        hh = sb("d_hh", [P, M, T], F32R)
        hl = sb("d_hl", [P, M, T], F32R)
        xin = sb("d_xin", [P, C, D], F32)
        sg = sb("d_sg", [P, 2, T], F32)
        h32 = sb("d_h32", [P, 2, T], F32)
        tmp = sb("d_tmp", [P, 2, D], F32)
        r = sb("d_r", [P, 2, D], F32)

        ps_t = ps("d_pst", [P, 2, KD, P])
        ps_g = ps("d_psg", [P, 2, T])
        ps_u = ps("d_psu", [P, 2, T])
        ps_o = ps("d_pso", [P, 2, D])

        s_small = sem("d_small")
        s_const = sem("d_const")
        s_prep, s_prep_down = sem("d_prep"), sem("d_prep_down")
        s_up_late, s_down = sem("d_up_late"), sem("d_down")
        s_x = [sem(f"d_x{c}") for c in range(C)]
        s_xt = sem("d_xt")
        s_xh = sem("d_xh")
        s_xl = sem("d_xl")
        s_g = sem("d_g")
        s_u = sem("d_u")
        s_sg = sem("d_sg")
        s_h = sem("d_h")
        s_hh = sem("d_hh")
        s_hl = sem("d_hl")
        s_dn = sem("d_dn")
        s_res = sem("d_res")
        s_var = sem("d_var")
        s_eps = sem("d_eps")
        s_std = sem("d_std")
        s_ln = sem("d_ln")
        s_chain = sem("d_chain")
        s_st = [sem(f"d_st{i}") for i in range(2)]
        s_r = [sem(f"d_r{i}") for i in range(2)]

        pieces = []
        for m in range(0, M, 2):
            cols = slice(m * P, (m + 2) * P)
            pieces.append((wg[:, :, cols], codes[2][:, :, cols], s_codes, codes[3]))
            if m < M // 2:
                pieces.append((wu_early[:, :, cols], codes[1][:, :, cols], s_codes, codes[3]))
            else:
                own = slice(m * P - half_ff, (m + 2) * P - half_ff)
                pieces.append((wu_late[:, :, own], wu_late_codes[:, :, own], s_up_late, 16 * KD))
        for m in range(0, M, 2):
            pieces.append((wd[:, m:m + 2, :], wd_codes[:, m:m + 2, :], s_down, 16 * KD))

        def gate_cols(k, m):
            return wg[:, k, m * P:(m + 1) * P]

        def up_cols(k, m):
            return wu_early[:, k, m * P:(m + 1) * P] if m < M // 2 else wu_late[:, k, m * P - half_ff:(m + 1) * P - half_ff]

        block = ctx.enter_context(nc.Block())

        @block.sync
        def _(sp):
            sp.dma_start(gs, gate_scale).then_inc(s_small, 16)
            sp.dma_start(us, up_scale).then_inc(s_small, 16)
            sp.dma_start(dsb, down_scale.partition_broadcast(P)).then_inc(s_small, 16)

            def chunk(dram, t, c):
                return dram[bass.ds(t * C + c, 1), :, :].rearrange("a p d -> p (a d)")

            def load_x(t):
                for c in range(C):
                    wait(sp, s_xt, C * t - C + c + 1)
                    sp.dma_start(xin[:, c, :], chunk(x_in, t, c)).then_inc(s_x[c], 16)

            def load_r(t, c):
                wait(sp, s_st[c % 2], 16 * (2 * t + c // 2))
                sp.dma_start(r[:, c % 2, :], chunk(x_in, t, c)).then_inc(s_r[c % 2], 16)

            load_x(0)
            for k in range(KD):
                sp.dma_start(wu_late_codes[:, k, :], up_wt[k * P:(k + 1) * P, half_ff:FF]).then_inc(s_up_late, 16)
            for k in range(KD):
                rows = slice(k * M // KD, (k + 1) * M // KD)
                sp.dma_start(wd_codes[:, rows, :], down_wt.rearrange("(m p) n -> p m n", p=P)[:, rows, :]).then_inc(s_down, 16)

            def step(t, more):
                if more:
                    load_x(t + 1)
                load_r(t, 0)
                load_r(t, 1)
                for c in range(C):
                    sp.wait_ge(s_ln, C * t + c + 1)
                    sp.dma_start(chunk(x_out, t, c), r[:, c % 2, :]).then_inc(s_st[c % 2], 16)
                    if c + 2 < C:
                        load_r(t, c + 2)

            pipelined(sp, NT, nothing, step)
            for i in range(2):
                sp.wait_ge(s_st[i], 16 * NT * C // 2)

        @block.gpsimd
        def _(pool):
            ident_fill(pool, ident, s_const)
            pool.memset(powers[:, 0:1], EPS)
            pool.memset(powers[:, 1:2], -0.5).then_inc(s_const, 1)

            def step(t, more):
                for m in range(M):
                    pool.wait_ge(s_hh, M * t + m + 1)
                    pool.tensor_tensor(hl[:, m, :], h32[:, m % 2, :], hh[:, m, :].bitcast(F32), ALU.subtract).then_inc(s_hl, 1)
                for c in range(C):
                    pool.wait_ge(s_var, C * t + c + 1)
                    root(pool, mv[:, c % 2, 1:2], powers, mv[:, c % 2, 2:3], s_eps, s_std, C * t + c + 1)

            pipelined(pool, NT, nothing, step)

        @block.scalar
        def _(act):
            act.wait_ge(s_small, 48)
            act.wait_ge(s_const, 3)

            def high(t, m):
                act.wait_ge(s_h, M * t + m + 1)
                act.activation(hh[:, m, :], h32[:, m % 2, :], ACT.Copy).then_inc(s_hh, 1)

            def front(t):
                for c in range(C):
                    act.wait_ge(s_xt, C * t + c + 1)
                    act.activation(xth[:, :, c * P:(c + 1) * P], ps_t[:, c % 2, :, :], ACT.Copy).then_inc(s_xh, 1)

            def step(t, more):
                for m in range(M):
                    act.wait_ge(s_g, M * t + m + 1)
                    wait(act, s_h, M * t + m - 1)
                    act.activation(sg[:, m % 2, :], ps_g[:, m % 2, :], ACT.Silu, scale=gs[:, m:m + 1]).then_inc(s_sg, 1)
                    if m:
                        high(t, m - 1)
                high(t, M - 1)
                if more:
                    front(t + 1)

            pipelined(act, NT, front, step)

        @block.vector
        def _(dve):
            def turn(i):
                dst, src, arrived, count = pieces[i]
                dve.wait_ge(arrived, count)
                dve.tensor_scalar(dst, src, -ZERO_POINT, None, ALU.add).then_inc(s_prep if i < M else s_prep_down, 1)

            turn(0)
            turn(1)
            dve.wait_ge(s_small, 48)

            def front(t):
                for c in range(C):
                    dve.wait_ge(s_xh, C * t + c + 1)
                    cols = slice(c * P, (c + 1) * P)
                    dve.tensor_tensor(xtl[:, :, cols], ps_t[:, c % 2, :, :], xth[:, :, cols].bitcast(F32), ALU.subtract).then_inc(s_xl, 1)

            def step(t, more):
                for m in range(M):
                    if isinstance(t, int) and t == 0:
                        if m % 2 == 0 and m + 2 < M:
                            turn(m + 2)
                            turn(m + 3)
                        if m >= M // 2:
                            turn(M + m - M // 2)
                    dve.wait_ge(s_sg, M * t + m + 1)
                    dve.wait_ge(s_u, M * t + m + 1)
                    wait(dve, s_hl, M * t + m - 1)
                    dve.scalar_tensor_tensor(out=h32[:, m % 2, :], in0=ps_u[:, m % 2, :], scalar=us[:, m:m + 1],
                                             in1=sg[:, m % 2, :], op0=ALU.mult, op1=ALU.mult).then_inc(s_h, 1)
                if more:
                    front(t + 1)
                link = chain(dve, s_chain, 2 * C * t)
                for c in range(C):
                    y = r[:, c % 2, :]
                    dve.wait_ge(s_dn, C * t + c + 1)
                    link(dve.tensor_tensor(tmp[:, c % 2, :], ps_o[:, c % 2, :], dsb, ALU.mult))
                    dve.wait_ge(s_r[c % 2], 16 * (2 * t + c // 2 + 1))
                    dve.tensor_tensor(y, y, tmp[:, c % 2, :], ALU.add).then_inc(s_res, 1)
                    dve.wait_ge(s_res, C * t + c + 1)
                    link(dve.bn_stats(stats[:, c % 2, :], y))
                    dve.memset(hold, 0.0)
                    dve.bn_aggr(mv[:, c % 2, 0:2], stats[:, c % 2, :]).then_inc(s_var, 1)
                    dve.wait_ge(s_std, C * t + c + 1)
                    dve.tensor_scalar(y, y, mv[:, c % 2, 0:1], mv[:, c % 2, 2:3], ALU.subtract, ALU.mult).then_inc(s_ln, 1)

            pipelined(dve, NT, front, step)

        @block.tensor
        def _(pe):
            pe.wait_ge(s_const, 3)

            def front(t):
                for c in range(C):
                    pe.wait_ge(s_x[c], 16 * t + 16)
                    wait(pe, s_xl, C * t + c - 1)
                    for k in range(KD):
                        last = pe.transpose(ps_t[:, c % 2, k, :], xin[:, c, k * P:(k + 1) * P], ident)
                    last.then_inc(s_xt, 1)

            def step(t, more):
                pe.wait_ge(s_xl, C * t + C)
                for m in range(M):
                    if isinstance(t, int) and t == 0 and m % 2 == 0:
                        pe.wait_ge(s_prep, m + 2)
                    for out, w, done, used in ((ps_g, gate_cols, s_g, s_sg), (ps_u, up_cols, s_u, s_h)):
                        wait(pe, used, M * t + m - 1)
                        for k in range(KD):
                            for x in (xth, xtl):
                                last = pe.matmul(out[:, m % 2, :], w(k, m), x[:, k, :],
                                                 start=(k == 0 and x is xth), stop=(k == KD - 1 and x is xtl))
                        last.then_inc(done, 1)
                if more:
                    front(t + 1)
                if isinstance(t, int) and t == 0:
                    pe.wait_ge(s_prep_down, len(pieces) - M)
                pe.wait_ge(s_hl, M * t + M)
                for c in range(C):
                    wait(pe, s_res, C * t + c - 1)
                    for m in range(M):
                        for h in (hh, hl):
                            last = pe.matmul(ps_o[:, c % 2, :], h[:, m, c * P:(c + 1) * P], wd[:, m, :],
                                             start=(m == 0 and h is hh), stop=(m == M - 1 and h is hl))
                    last.then_inc(s_dn, 1)

            pipelined(pe, NT, front, step)


def fill_identity(pool, ident, done):
    pool.memset(ident, 0.0).then_inc(done, 1)
    pool.wait_ge(done, 1)
    pool.affine_select(out=ident, in_=ident, compare_op=ALU.not_equal, fill=1.0, base=0,
                       pattern=[[-1, P]], channel_multiplier=1).then_inc(done, 1)


def build(nc, x, out, d):
    between = [nc.dram_tensor(f"tokens{i}", x.shape, F32, kind="Internal").ap() for i in range(3)]
    signals = Signals(nc)
    mamba2(nc, signals, x, between[0], d["w_x"], d["w_bc"], d["w_gate"], d["w_out0"], d["conv0"], d["A_log"], d["dt_bias"],
           d["D_skip"], d["norm_w"], fill_identity)
    signals.reset()
    w_place, raw_start = Sbuf(nc, SBUF_START, SBUF_END), SBUF_END - 4 * 5 * KD * D
    raw = Sbuf(nc, raw_start, SBUF_END)("c_raw", [P, 5, KD, D], F32)
    weights, W, split = [], {}, []
    for i, (n, name) in enumerate((("x", "w_in1"), ("y", "w_y"), ("ig", "w_ig"), ("ag", "w_ag"), ("out", "w_out1"))):
        W[n] = tuple(w_place(f"c_w{n}{part}", [P, KD, D], F32R) for part in "hl")
        arrived = signals(f"c_raw_{n}")
        weights.append((raw[:, i], d[name].rearrange("(k p) n -> p k n", p=P), arrived))
        split.append((raw[:, i], arrived, *W[n]))
    codes, transfers = ffn_codes(nc, d["gate_w"], d["up_w"])
    s_codes = signals("d_codes")
    bounded_ffn(nc, signals, between[0], between[1], d["weight"], d["scale"], fill_identity, (w_place.at, raw_start), weights, split)
    rg_lru(nc, signals, between[1], between[2], d["vectors"], d["b_out"], fill_identity, W, (w_place.at, codes[0]),
           [(dst, src, s_codes) for dst, src in transfers])
    gated_ffn(nc, signals, between[2], out, d["gate_w"], d["up_w"], d["down_w"], d["gate_scale"], d["up_scale"], d["down_scale"],
              fill_identity, codes, s_codes)


def kernel(**inputs):
    import numpy as np
    import concourse.bacc as bacc
    from concourse.bass_utils import run_bass_kernel_spmd as run

    v = {name: np.asarray(a) for name, a in inputs.items()}
    nc = bacc.Bacc("TRN2", target_bir_lowering=False, num_devices=1)
    arrays, d = {}, {}

    def dram(name, a):
        a = np.ascontiguousarray(a)
        arrays["in_" + name] = a
        d[name] = nc.dram_tensor("in_" + name, a.shape, mybir.dt.from_np(a.dtype), kind="ExternalInput").ap()

    x = v["L0_attn_hidden_states"]
    dram("x", x.reshape(-1, P, D))

    w_in, conv_w, conv_b = v["L0_attn_W_in"], v["L0_attn_conv_w"], v["L0_attn_conv_b"]
    di, n, h = v["L0_attn_norm_w"].shape[0], 16, v["L0_attn_A_log"].shape[0]
    gap = np.zeros((D, 32 - n), w_in.dtype)
    dram("w_gate", w_in[:, :di])
    dram("w_x", w_in[:, di:2 * di])
    dram("w_bc", np.concatenate([w_in[:, 2 * di:2 * di + n], gap, w_in[:, 2 * di + n:2 * di + 2 * n], gap,
                                 w_in[:, 2 * di + 2 * n:], np.zeros((D, P - 64 - h), w_in.dtype)], axis=1))
    taps = np.concatenate([conv_w, conv_b[:, None]], axis=1)
    none = np.zeros((32 - n, taps.shape[1]), taps.dtype)
    rows = np.concatenate([taps[:di + n], none, taps[di + n:], none, np.zeros((64, taps.shape[1]), taps.dtype)])
    dram("conv0", rows.reshape(-1, P, taps.shape[1]).transpose(1, 0, 2))
    for name in ("A_log", "dt_bias", "D_skip"):
        dram(name, v["L0_attn_" + name])
    dram("norm_w", v["L0_attn_norm_w"].reshape(-1, P).T)
    dram("w_out0", v["L0_attn_W_out"])

    dram("weight", v["L0_ffn_weight"])
    dram("scale", v["L0_ffn_scale"])

    for name, key in (("w_in1", "w_x"), ("w_y", "w_y"), ("w_ig", "w_ig"), ("w_ag", "w_ag"), ("w_out1", "w_out"), ("b_out", "b_out")):
        dram(name, v["L1_attn_" + key])
    vectors = np.concatenate([np.stack([v["L1_attn_" + k] for k in ("b_x", "b_y", "b_ig", "b_ag", "conv_b", "a_param")]),
                              v["L1_attn_conv_w"]])
    dram("vectors", vectors.reshape(vectors.shape[0], KD, P).transpose(2, 0, 1))

    for name in ("gate_w", "up_w", "down_w"):
        dram(name, v["L1_ffn_" + name].T)
    for name in ("gate_scale", "up_scale"):
        dram(name, v["L1_ffn_" + name].reshape(-1, P).T)
    dram("down_scale", v["L1_ffn_down_scale"])

    out = nc.dram_tensor("out", arrays["in_x"].shape, F32, kind="ExternalOutput").ap()
    build(nc, d["x"], out, d)
    r = run(nc, [arrays], core_ids=[0])
    return r.results[0]["out"].reshape(x.shape)
```
